# Optimizing a Trainium2 kernel written in Bass

```python
import numpy as np
import jax
import jax.numpy as jnp

def _softmax(x, axis=-1):
    return jax.nn.softmax(x, axis=axis)

def _gelu(x):
    return jax.nn.gelu(x, approximate=True)

def _silu(x):
    return jax.nn.silu(x)

def _sigmoid(x):
    return jax.nn.sigmoid(x)

def _layernorm(x, axis=-1, eps=1e-05):
    m = jnp.mean(x, axis=axis, keepdims=True)
    v = jnp.var(x, axis=axis, keepdims=True)
    return (x - m) / jnp.sqrt(v + eps)

def _scatter_add(tgt, idx, src, axis=0):
    return tgt.at[idx].add(src)

def _segment_sum(src, seg, n):
    return jax.ops.segment_sum(src, seg, n)
kernel_name = 'mk_lm_tower_d1_tok_ids2048_r4_9703bc'

def setup_inputs(seed: int=0):
    np.random.seed(seed)
    _w = jnp.asarray

    def _rec_inputs():
        import jax
        import jax.numpy as jnp
        _rk = jax.random.key(seed)
        x = jax.random.randint(jax.random.fold_in(_rk, 1), (2, 1024), 0, 12564, jnp.int32)
        return x
    x = _rec_inputs()

    def _L0_tok_setup():
        import jax, jax.numpy as jnp
        import numpy as np
        VOCAB, DIM, RANK = (50257, 512, 16)
        ALPHA = 32.0
        SCALING = ALPHA / RANK
        key = jax.random.key(seed)
        k1, k2, k3, k4 = jax.random.split(key, 4)
        input_ids = jax.random.randint(k1, (4, 1024), 0, VOCAB, dtype=jnp.int64)
        W = jax.random.normal(k2, (VOCAB, DIM), dtype=jnp.float32) * 0.02
        lora_A = jax.random.normal(k3, (RANK, VOCAB), dtype=jnp.float32) * 0.02
        lora_B = jax.random.normal(k4, (DIM, RANK), dtype=jnp.float32)
        return {'input_ids': input_ids, 'W': W, 'lora_A': lora_A, 'lora_B': lora_B}
    _L0_tok_all = _L0_tok_setup()
    _L0_tok_in = {k: v for k, v in _L0_tok_all.items() if k in ('W', 'lora_A', 'lora_B')}
    del _L0_tok_all

    def _L0_attn_setup():
        import jax, jax.numpy as jnp
        import numpy as np
        B, N, H = (2, 1024, 512)
        NH, HD = (16, 128)
        BLK = 64
        EPS = 1e-06

        def _lightning_attn(x, slope_rate, w_qkv, w_gate, w_out, norm_w):
            b, n, _ = x.shape
            h, d = (NH, HD)
            nb = n // BLK
            qkv = jax.nn.silu(jnp.einsum('bnf,of->bno', x, w_qkv))
            qkv = qkv.reshape(b, n, h, 3 * d)
            q, k, v = jnp.split(qkv, 3, axis=-1)
            q = q.transpose(0, 2, 1, 3)
            k = k.transpose(0, 2, 1, 3)
            v = v.transpose(0, 2, 1, 3)
            s = slope_rate.astype(jnp.float32)
            arr = jnp.arange(1, BLK + 1, dtype=jnp.float32)
            q_decay = jnp.exp(-s * arr[:, None])
            k_decay = jnp.exp(-s * (BLK - arr)[:, None])
            idx = arr[:, None] - arr[None, :]
            diag_decay = jnp.where(idx >= 0, jnp.exp(-s * idx), 0.0)
            block_decay = jnp.exp(-s * BLK)
            qb = q.reshape(b, h, nb, BLK, d).transpose(2, 0, 1, 3, 4)
            kb = k.reshape(b, h, nb, BLK, d).transpose(2, 0, 1, 3, 4)
            vb = v.reshape(b, h, nb, BLK, d).transpose(2, 0, 1, 3, 4)

            def step(kv, blk):
                qi, ki, vi = blk
                o_inter = jnp.einsum('bhmd,bhde->bhme', qi * q_decay, kv)
                qk = jnp.einsum('bhmd,bhnd->bhmn', qi, ki) * diag_decay
                o_intra = jnp.einsum('bhmn,bhne->bhme', qk, vi)
                kv_new = block_decay * kv + jnp.einsum('bhmd,bhme->bhde', ki * k_decay, vi)
                return (kv_new, o_inter + o_intra)
            kv0 = jnp.zeros((b, h, d, d), dtype=jnp.float32)
            _, out = jax.lax.scan(step, kv0, (qb, kb, vb))
            out = out.transpose(1, 2, 0, 3, 4).reshape(b, h, n, d)
            out = out.transpose(0, 2, 1, 3).reshape(b, n, h * d)
            var = jnp.mean(out * out, axis=-1, keepdims=True)
            out = norm_w * (out * jax.lax.rsqrt(var + EPS))
            gate = jax.nn.sigmoid(jnp.einsum('bnf,of->bno', x, w_gate))
            return jnp.einsum('bno,fo->bnf', gate * out, w_out)
        key = jax.random.key(seed)
        ks = jax.random.split(key, 5)
        scale = 0.02
        x = jax.random.normal(ks[0], (B, N, H), dtype=jnp.float32)
        slopes = (1.0 / 2.0 ** (8.0 * np.arange(1, NH + 1) / NH)).astype(np.float32)
        slope_rate = jnp.asarray(slopes).reshape(NH, 1, 1)
        w_qkv = jax.random.normal(ks[1], (3 * NH * HD, H), dtype=jnp.float32) * scale
        w_gate = jax.random.normal(ks[2], (NH * HD, H), dtype=jnp.float32) * scale
        w_out = jax.random.normal(ks[3], (H, NH * HD), dtype=jnp.float32) * scale
        norm_w = jnp.ones((NH * HD,), dtype=jnp.float32)
        return {'hidden_states': x, 'slope_rate': slope_rate, 'w_qkv': w_qkv, 'w_gate': w_gate, 'w_out': w_out, 'norm_w': norm_w}
    _L0_attn_all = _L0_attn_setup()
    _L0_attn_in = {k: v for k, v in _L0_attn_all.items() if k in ('slope_rate', 'w_qkv', 'w_gate', 'w_out', 'norm_w')}
    del _L0_attn_all

    def _L0_ffn_setup():
        import jax, jax.numpy as jnp
        import numpy as np
        DIM_IN = 512
        DIM_HIDDEN = 2048
        key = jax.random.key(seed)
        k_x, k_g, k_u, k_d = jax.random.split(key, 4)
        s_in = 1.0 / np.sqrt(DIM_IN)
        s_hid = 1.0 / np.sqrt(DIM_HIDDEN)
        x = jax.random.normal(k_x, (4, 512, DIM_IN), dtype=jnp.float32)
        w_gate = jax.random.uniform(k_g, (DIM_HIDDEN, DIM_IN), jnp.float32, -s_in, s_in)
        w_up = jax.random.uniform(k_u, (DIM_HIDDEN, DIM_IN), jnp.float32, -s_in, s_in)
        w_down = jax.random.uniform(k_d, (DIM_IN, DIM_HIDDEN), jnp.float32, -s_hid, s_hid)
        return {'x': x, 'w_gate': w_gate, 'w_up': w_up, 'w_down': w_down}
    _L0_ffn_all = _L0_ffn_setup()
    _L0_ffn_in = {k: v for k, v in _L0_ffn_all.items() if k in ('w_gate', 'w_up', 'w_down')}
    del _L0_ffn_all
    return {'x': x, 'L0_tok_W': _L0_tok_in['W'], 'L0_tok_lora_A': _L0_tok_in['lora_A'], 'L0_tok_lora_B': _L0_tok_in['lora_B'], 'L0_attn_slope_rate': _L0_attn_in['slope_rate'], 'L0_attn_w_qkv': _L0_attn_in['w_qkv'], 'L0_attn_w_gate': _L0_attn_in['w_gate'], 'L0_attn_w_out': _L0_attn_in['w_out'], 'L0_attn_norm_w': _L0_attn_in['norm_w'], 'L0_ffn_w_gate': _L0_ffn_in['w_gate'], 'L0_ffn_w_up': _L0_ffn_in['w_up'], 'L0_ffn_w_down': _L0_ffn_in['w_down']}

def reference(x, L0_tok_W, L0_tok_lora_A, L0_tok_lora_B, L0_attn_slope_rate, L0_attn_w_qkv, L0_attn_w_gate, L0_attn_w_out, L0_attn_norm_w, L0_ffn_w_gate, L0_ffn_w_up, L0_ffn_w_down):
    import jax
    import jax.numpy as jnp

    def _L0_tok_ref(input_ids, W, lora_A, lora_B):
        import jax, jax.numpy as jnp
        import numpy as np
        VOCAB, DIM, RANK = (50257, 512, 16)
        ALPHA = 32.0
        SCALING = ALPHA / RANK
        base = jnp.take(W, input_ids, axis=0)
        a_tok = jnp.take(lora_A, input_ids, axis=1)
        delta = jnp.einsum('rbs,dr->bsd', a_tok, lora_B)
        return base + delta * SCALING

    def _L0_attn_ref(hidden_states, slope_rate, w_qkv, w_gate, w_out, norm_w):
        import jax, jax.numpy as jnp
        import numpy as np
        B, N, H = (2, 1024, 512)
        NH, HD = (16, 128)
        BLK = 64
        EPS = 1e-06

        def _lightning_attn(x, slope_rate, w_qkv, w_gate, w_out, norm_w):
            b, n, _ = x.shape
            h, d = (NH, HD)
            nb = n // BLK
            qkv = jax.nn.silu(jnp.einsum('bnf,of->bno', x, w_qkv))
            qkv = qkv.reshape(b, n, h, 3 * d)
            q, k, v = jnp.split(qkv, 3, axis=-1)
            q = q.transpose(0, 2, 1, 3)
            k = k.transpose(0, 2, 1, 3)
            v = v.transpose(0, 2, 1, 3)
            s = slope_rate.astype(jnp.float32)
            arr = jnp.arange(1, BLK + 1, dtype=jnp.float32)
            q_decay = jnp.exp(-s * arr[:, None])
            k_decay = jnp.exp(-s * (BLK - arr)[:, None])
            idx = arr[:, None] - arr[None, :]
            diag_decay = jnp.where(idx >= 0, jnp.exp(-s * idx), 0.0)
            block_decay = jnp.exp(-s * BLK)
            qb = q.reshape(b, h, nb, BLK, d).transpose(2, 0, 1, 3, 4)
            kb = k.reshape(b, h, nb, BLK, d).transpose(2, 0, 1, 3, 4)
            vb = v.reshape(b, h, nb, BLK, d).transpose(2, 0, 1, 3, 4)

            def step(kv, blk):
                qi, ki, vi = blk
                o_inter = jnp.einsum('bhmd,bhde->bhme', qi * q_decay, kv)
                qk = jnp.einsum('bhmd,bhnd->bhmn', qi, ki) * diag_decay
                o_intra = jnp.einsum('bhmn,bhne->bhme', qk, vi)
                kv_new = block_decay * kv + jnp.einsum('bhmd,bhme->bhde', ki * k_decay, vi)
                return (kv_new, o_inter + o_intra)
            kv0 = jnp.zeros((b, h, d, d), dtype=jnp.float32)
            _, out = jax.lax.scan(step, kv0, (qb, kb, vb))
            out = out.transpose(1, 2, 0, 3, 4).reshape(b, h, n, d)
            out = out.transpose(0, 2, 1, 3).reshape(b, n, h * d)
            var = jnp.mean(out * out, axis=-1, keepdims=True)
            out = norm_w * (out * jax.lax.rsqrt(var + EPS))
            gate = jax.nn.sigmoid(jnp.einsum('bnf,of->bno', x, w_gate))
            return jnp.einsum('bno,fo->bnf', gate * out, w_out)
        return _lightning_attn(hidden_states, slope_rate, w_qkv, w_gate, w_out, norm_w)

    def _L0_ffn_ref(x, w_gate, w_up, w_down):
        import jax, jax.numpy as jnp
        import numpy as np
        DIM_IN = 512
        DIM_HIDDEN = 2048
        gate = jnp.einsum('bsd,hd->bsh', x, w_gate)
        up = jnp.einsum('bsd,hd->bsh', x, w_up)
        gated = jax.nn.silu(gate) * up
        return jnp.einsum('bsh,dh->bsd', gated, w_down)
    h = _L0_tok_ref(x, L0_tok_W, L0_tok_lora_A, L0_tok_lora_B)
    h = h + _L0_attn_ref(_layernorm(h, axis=-1), L0_attn_slope_rate, L0_attn_w_qkv, L0_attn_w_gate, L0_attn_w_out, L0_attn_norm_w)
    h = h + _L0_ffn_ref(_layernorm(h, axis=-1), L0_ffn_w_gate, L0_ffn_w_up, L0_ffn_w_down)
    return h

_drawn_inputs = setup_inputs


def setup_inputs(seed=0):
    import zlib

    import numpy as np

    out = dict(_drawn_inputs(seed))
    spreads = {'L0_attn_norm_w': (1.0, 0.2)}
    factors = {}
    for name, (base, spread) in spreads.items():
        noise = np.random.default_rng([zlib.crc32(name.encode()), seed]).standard_normal(out[name].shape)
        drawn = base * np.exp(spread * noise) if base else spread * noise
        out[name] = jnp.asarray(drawn.astype(out[name].dtype))
    for name, factor in factors.items():
        out[name] = (out[name] * factor).astype(out[name].dtype)
    return out
```

```python
from contextlib import ExitStack

import numpy as np
import concourse.bass as bass
from concourse import mybir
from concourse.alu_op_type import AluOpType as ALU

F32 = mybir.dt.float32
F32R = mybir.dt.float32r
I32 = mybir.dt.int32
ACT = mybir.ActivationFunctionType

P = 128
D = 512
KC = D // P
T = 2048
TILES = T // P
BLOCK = 512
BT = BLOCK // P
BLOCKS = T // BLOCK
SEQ_TILES = 1024 // P
HEADS = 16
INNER = HEADS * P
CHUNKS = 2048 // P
RANK = 16
SCALING = 32.0 / RANK
LN_EPS = 1e-5
RMS_EPS = 1e-6
STEPS = HEADS * BLOCKS
F_STEPS = CHUNKS * BLOCKS
PEELED = 2
SCANS = SEQ_TILES - 1
LN_OPS = 8
TAB = 2 * P + 1
DMA = 16


class Step:

    def __init__(self, i, k):
        self.s = BLOCKS * i + k
        self.done = self.s + 1
        self.tc = k % BLOCKS
        self.head = i + k // BLOCKS
        self.second = self.tc % 2
        self.seq = 2 * self.head + self.tc // 2
        self.first_ever = isinstance(self.s, int) and self.s == 0
        self.later = not isinstance(self.s, int) or self.s > 1
        self.last_head = isinstance(self.head, int) and self.head == HEADS - 1


def build(nc, ids, table, lora_a, lora_b, slopes, norm_w, w_qkv, w_gate, w_out, f_gate, f_up, f_down, h_spill, out):
    with ExitStack() as ctx:
        def sb(name, shape, dt=F32):
            return ctx.enter_context(nc.sbuf_tensor(name, shape, dt))

        def sem(name):
            return ctx.enter_context(nc.semaphore(name))

        acc = sb("acc", [P, TILES, D])
        xn_hi = sb("xn_hi", [P, KC, T], F32R)
        xn_lo = sb("xn_lo", [P, KC, T], F32R)
        ssq = sb("ssq", [P, T])
        tab = sb("tab", [P, HEADS, TAB])
        slope = sb("slope", [P, HEADS])
        normw = sb("normw", [P, HEADS])
        ident = sb("ident", [P, P])
        ones2 = sb("ones2", [P, 2])
        raw = {n: sb(f"{n}_raw", [P, D]) for n in "kvqgo"}
        w_hi = {n: sb(f"{n}_whi", [P, D], F32R) for n in "kvqgo"}
        w_lo = {n: sb(f"{n}_wlo", [P, D], F32R) for n in "kvqgo"}
        k32, v32, q32, qd32, st32, o32, gate, sq = (
            sb(n, [P, BLOCK]) for n in ("k32", "v32", "q32", "qd32", "st32", "o32", "gate", "sq"))
        state = sb("state", [P, SEQ_TILES, P])
        names = ("q", "qd", "kT", "k", "v", "st", "s", "o")
        hi = {n: sb(f"{n}_hi", [P, BLOCK], F32R) for n in names}
        lo = {n: sb(f"{n}_lo", [P, BLOCK], F32R) for n in names}
        idx = sb("idx", [P, TILES], I32)
        a_tok = sb("a_tok", [P, 4, RANK])
        aT = sb("aT", [RANK, 2, P])
        stats = sb("stats", [P, 2, 6])
        mv = sb("mv", [P, 2, 2])
        var, std, rstd0, newton, rstd = (sb(n, [P, 2]) for n in ("var", "std", "rstd0", "newton", "rstd"))
        o_var, o_std, o_r0, o_newton, o_r = (
            sb(n, [P, TILES]) for n in ("o_var", "o_std", "o_r0", "o_newton", "o_r"))
        loraB = st32
        iota_i = o32[:, 0:TAB].bitcast(I32)
        iota_f = gate[:, 0:TAB]
        xn = (k32, v32)
        h_in = (q32, qd32)

        A, B, TK, TV, ST, KV, O, Y3 = (
            ctx.enter_context(nc.psum_tensor(f"bank_{n}", [P, BLOCK], F32))
            for n in ("a", "b", "tk", "tv", "st", "kv", "o", "y3"))
        y_bank = (ST, KV, O, Y3)

        consts_in, const_step, exponents, tables, masked, ssq_zero = (
            sem(n) for n in ("consts_in", "const_step", "exponents", "tables", "masked", "ssq_zero"))
        gathered = [sem(f"gathered{u}") for u in range(4)]
        a_turned, aT_ready, delta_done, h_ready, acc_zero = (
            sem(n) for n in ("a_turned", "aT_ready", "delta_done", "h_ready", "acc_zero"))
        h_spilled = [sem(f"h_spilled{u}") for u in range(4)]
        h_back = [sem(f"h_back{u}") for u in range(2)]
        ln_op, var_ready, std_ready, xn_ready, xn_turned, xn_hi_done, xn_lo_done = (
            sem(n) for n in ("ln_op", "var_ready", "std_ready", "xn_ready", "xn_turned", "xn_hi_done", "xn_lo_done"))
        ss_summed, o_var_ready, o_std_ready, o_rms_op = (
            sem(n) for n in ("ss_summed", "o_var_ready", "o_std_ready", "o_rms_op"))

        loaded = {n: sem(f"loaded_{n}") for n in "kvqgo"}
        w_hi_done = {n: sem(f"w_hi_done_{n}") for n in "kvqgo"}
        w_ready = {n: sem(f"w_ready_{n}") for n in "kvqgo"}

        proj = {n: sem(f"proj_{n}") for n in "kvqg"}
        silu = {n: sem(f"silu_{n}") for n in "kvq"}
        k_turned, v_turned, scores_done, kv_done, o_done, y_done = (
            sem(n) for n in ("k_turned", "v_turned", "scores_done", "kv_done", "o_done", "y_done"))
        hi_done = {n: sem(f"hi_done_{n}") for n in names}
        lo_done = {n: sem(f"lo_done_{n}") for n in names}
        gate_done, sq_done, ssq_added, o_gated, y_added, st_masked, states, qd_done = (
            sem(n) for n in ("gate_done", "sq_done", "ssq_added", "o_gated",
                             "y_added",
                             "st_masked",
                             "states",
                             "qd_done"))
        fg_proj, fu_proj, f_silu, f_mul, f_hi, f_lo, d_done, d_free, out_done = (
            sem(n) for n in ("fg_proj", "fu_proj", "f_silu", "f_mul", "f_hi", "f_lo",
                             "d_done",
                             "d_free",
                             "out_done"))

        block = ctx.enter_context(nc.Block())

        def settled(eng, count):
            if not isinstance(count, int):
                eng.lower_val(count)
            return count

        def wait_apart(eng, semaphore, count, least=1):
            count = settled(eng, count)
            eng.wait_ge(semaphore, least)
            eng.wait_ge(semaphore, count)

        def tile(ap, c):
            return ap[:, c * P:(c + 1) * P]

        def four(ap):
            return ap[:, :].rearrange("p (c n) -> p c n", c=BT)

        def column(t, c):
            return t[:, bass.ds(c, 1)]

        def acc_tile(t):
            return acc[:, bass.ds(t, 1), :].rearrange("p a d -> p (a d)")

        def kdecay(c):
            return tab[:, bass.ds(c.head, 1), 2 * P:TAB].rearrange("p a b -> p (a b)")

        def cdecay(c):
            return tab[:, bass.ds(c.head, 1), 2 * P - 1:2 * P].rearrange("p a b -> p (a b)")

        def state_parts(c):
            return (0, BT) if c.second else (1, 1)

        def f_banks(c):
            return (TK, TV) if c.tc % 2 else (A, B)

        attn_src = {"q": lambda h: w_qkv[0, h], "k": lambda h: w_qkv[1, h], "v": lambda h: w_qkv[2, h],
                    "g": lambda h: w_gate[h], "o": lambda h: w_out[h]}
        ffn_src = {"k": lambda j: f_gate[j], "v": lambda j: f_up[j], "o": lambda j: f_down[j]}

        @block.sync
        def _(sp):
            sp.dma_start(idx[:, :], ids).then_inc(consts_in, DMA)
            sp.dma_start(slope[:, :], slopes.broadcast_to([P, HEADS])).then_inc(consts_in, DMA)
            sp.dma_start(loraB[0:RANK, :], lora_b).then_inc(consts_in, DMA)
            sp.dma_start(normw[:, :], norm_w).then_inc(consts_in, DMA)
            for n in "kvqgo":
                sp.dma_start(raw[n][:, :], attn_src[n](0)).then_inc(loaded[n], DMA)

            with sp.Fori(0, TILES // 4) as i:
                for u in range(4):
                    t = 4 * i + u
                    wait_apart(sp, h_ready, t + 1)
                    sp.dma_start(h_spill[bass.ds(t, 1)].rearrange("a p d -> (a p) d"),
                                 acc_tile(t)).then_inc(h_spilled[u], DMA)
                for u in range(4):
                    wait_apart(sp, h_spilled[u], DMA * (i + 1), DMA)

            with sp.Fori(1, HEADS) as h:
                for n in "kvqgo":
                    wait_apart(sp, w_ready[n], h)
                    sp.dma_start(raw[n][:, :], attn_src[n](bass.ds(h, 1)).rearrange("a p n -> (a p) n")
                                 ).then_inc(loaded[n], DMA)
            for n in "kvo":
                sp.wait_ge(w_ready[n], HEADS)
                sp.dma_start(raw[n][:, :], ffn_src[n](0)).then_inc(loaded[n], DMA)

            sp.wait_ge(lo_done["q"], STEPS)
            sp.wait_ge(lo_done["qd"], STEPS)
            with sp.Fori(0, TILES // 2) as i:
                for u in range(2):
                    t = 2 * i + u
                    sp.wait_ge(h_ready, TILES + t - 1)
                    sp.dma_start(h_in[u][:, :], h_spill[bass.ds(t, 1)].rearrange("a p d -> (a p) d")
                                 ).then_inc(h_back[u], DMA)

            with sp.Fori(1, CHUNKS) as j:
                for n in "kvo":
                    sp.wait_ge(w_ready[n], HEADS + j)
                    sp.dma_start(raw[n][:, :], ffn_src[n](bass.ds(j, 1)).rearrange("a p n -> (a p) n")
                                 ).then_inc(loaded[n], DMA)
            for t in range(TILES):
                sp.wait_ge(d_free, BT * F_STEPS - TILES + BT + t + 1)
                sp.dma_start(out[t * P:(t + 1) * P, :], acc[:, t, :]).then_inc(out_done, DMA)
            sp.wait_ge(out_done, DMA * TILES)

        def split_weights(pool, n, count, used=None, uses=None):
            if used is not None:
                uses = settled(pool, uses)
            wait_apart(pool, loaded[n], DMA * count, DMA)
            if used is not None:
                pool.wait_ge(used, uses)
            nc.gpsimd.tensor_copy(w_hi[n][:, :], raw[n][:, :]).then_inc(w_hi_done[n], 1)
            wait_apart(pool, w_hi_done[n], count)
            nc.gpsimd.tensor_tensor(w_lo[n][:, :], raw[n][:, :], w_hi[n][:, :].bitcast(F32),
                                    ALU.subtract).then_inc(w_ready[n], 1)

        @block.gpsimd
        def _(pool):
            nc.gpsimd.memset(ident[:, :], 0.0).then_inc(const_step, 1)
            nc.gpsimd.memset(ones2[:, :], 1.0).then_inc(const_step, 1)
            nc.gpsimd.iota(iota_i[:, 0:P], pattern=[[-1, P]], base=0, channel_multiplier=1).then_inc(exponents, 1)
            nc.gpsimd.iota(iota_i[:, P:2 * P], pattern=[[-1, P]], base=-1, channel_multiplier=0
                           ).then_inc(exponents, 1)
            nc.gpsimd.iota(iota_i[:, 2 * P:TAB], pattern=[[1, 1]], base=1 - P, channel_multiplier=1
                           ).then_inc(exponents, 1)
            pool.wait_ge(exponents, 3)
            nc.gpsimd.tensor_scalar(iota_f, iota_i, 0.0, None, ALU.min).then_inc(exponents, 1)
            pool.wait_ge(const_step, 2)
            nc.gpsimd.affine_select(out=ident[:, :], in_=ident[:, :], compare_op=ALU.not_equal, fill=1.0, base=0,
                                    pattern=[[-1, P]], channel_multiplier=1).then_inc(const_step, 1)
            pool.wait_ge(consts_in, 4 * DMA)
            for t in range(TILES):
                u = t % 4
                if t >= 4:
                    pool.wait_ge(gathered[u], 2 * DMA * (t // 4))
                    pool.wait_ge(a_turned, t - 3)
                nc.gpsimd.indirect_dma_start(acc[:, t, :], None, table[:, :],
                                             bass.IndirectOffsetOnAxis(idx[:, t:t + 1], 0)
                                             ).then_inc(gathered[u], DMA)
                nc.gpsimd.indirect_dma_start(a_tok[:, u, :], None, lora_a[:, :],
                                             bass.IndirectOffsetOnAxis(idx[:, t:t + 1], 0)
                                             ).then_inc(gathered[u], DMA)
            pool.wait_ge(tables, HEADS)
            nc.gpsimd.affine_select(out=tab[:, :, 0:P], in_=tab[:, :, 0:P], compare_op=ALU.is_ge, fill=0.0, base=0,
                                    pattern=[[0, HEADS], [1, P]], channel_multiplier=-1).then_inc(masked, 1)
            nc.gpsimd.memset(ssq[:, :], 0.0).then_inc(ssq_zero, 1)
            for n in "kvqgo":
                split_weights(pool, n, 1)
            for t in range(TILES):
                pool.wait_ge(h_spilled[t % 4], DMA * (t // 4 + 1))
                pool.wait_ge(xn_ready, t + 1)
                nc.gpsimd.memset(acc[:, t, :], 0.0).then_inc(acc_zero, 1)
            pool.wait_ge(ssq_zero, 1)

            def add_squares(p):
                cols = ssq[:, p.tc * BLOCK:(p.tc + 1) * BLOCK]
                pool.wait_ge(sq_done, p.done)
                nc.gpsimd.tensor_tensor(cols, cols, sq[:, :], ALU.add).then_inc(ssq_added, 1)

            def slot(i, k):
                c = Step(i, k)
                renew = c.tc == BLOCKS - 1 and not c.last_head
                if not c.first_ever:
                    add_squares(Step(i, k - 1))
                if renew:
                    for n in "kv":
                        split_weights(pool, n, c.head + 2, proj[n], c.done)
                wait_apart(pool, silu["q"], c.done)
                decay = tab[:, bass.ds(c.head, 1), P:2 * P].broadcast_to([P, BT, P])
                nc.gpsimd.tensor_tensor(four(qd32), four(q32), decay, ALU.mult).then_inc(qd_done, 1)
                wait_apart(pool, qd_done, c.done)
                if not c.first_ever:
                    pool.wait_ge(o_done, c.s)
                nc.gpsimd.tensor_copy(hi["qd"][:, :], qd32[:, :]).then_inc(hi_done["qd"], 1)
                pool.wait_ge(hi_done["qd"], c.done)
                nc.gpsimd.tensor_tensor(lo["qd"][:, :], qd32[:, :], hi["qd"][:, :].bitcast(F32),
                                        ALU.subtract).then_inc(lo_done["qd"], 1)
                if renew:
                    for n in "qg":
                        split_weights(pool, n, c.head + 2, proj[n], c.done)
                if c.tc == 0 and not c.first_ever:
                    split_weights(pool, "o", c.head + 1, y_done, BT * c.s)

            for k in range(PEELED):
                slot(0, k)
            with pool.Fori(0, HEADS - 1) as i:
                for k in range(PEELED, PEELED + BLOCKS):
                    slot(i, k)
            for k in range(PEELED, BLOCKS):
                slot(HEADS - 1, k)
            add_squares(Step(HEADS - 1, BLOCKS - 1))
            pool.wait_ge(y_done, BT * STEPS)
            for n in "kvo":
                split_weights(pool, n, HEADS + 1)

            with pool.Fori(0, CHUNKS - 1) as j:
                last = Step(j, BLOCKS - 1)
                for n, used in (("k", fg_proj), ("v", fu_proj)):
                    split_weights(pool, n, HEADS + j + 2, used, last.done)
                split_weights(pool, "o", HEADS + j + 2, d_done, BT * last.done)

        @block.scalar
        def _(act):
            act.wait_ge(exponents, 4)
            act.wait_ge(consts_in, 4 * DMA)
            for h in range(HEADS):
                nc.scalar.activation(tab[:, h, :], iota_f, ACT.Exp, scale=slope[:, h:h + 1]).then_inc(tables, 1)

            def part_of_xn(t, u):
                cols = xn_hi[:, :, bass.ds(P * t, P)]
                act.wait_ge(xn_turned, off + t + 1)
                nc.scalar.copy(cols, four((ST, KV)[u % 2])).then_inc(xn_hi_done, 1)

            def root(t, u):
                act.wait_ge(var_ready, off + t + 1)
                nc.scalar.activation(std[:, u % 2:u % 2 + 1], var[:, u % 2:u % 2 + 1], ACT.Sqrt
                                     ).then_inc(std_ready, 1)

            off = 0
            with act.Fori(0, TILES // 4) as i:
                for u in range(4):
                    t = 4 * i + u
                    act.wait_ge(a_turned, t + 1)
                    nc.scalar.copy(aT[:, u % 2, :], (A, B)[u % 2][0:RANK, 0:P]).then_inc(aT_ready, 1)
                    root(t, u)
                    if u:
                        part_of_xn(t - 1, u - 1)
                part_of_xn(4 * i + 3, 3)

            def squares(p):
                act.wait_ge(o_gated, p.done)
                if not p.first_ever:
                    act.wait_ge(ssq_added, p.s)
                nc.scalar.activation(sq[:, :], O[:, :], ACT.Square).then_inc(sq_done, 1)

            def o_high(p):
                if not p.first_ever:
                    act.wait_ge(y_done, BT * p.s)
                nc.scalar.copy(hi["o"][:, :], o32[:, :]).then_inc(hi_done["o"], 1)

            def slot(i, k):
                c = Step(i, k)
                act.wait_ge(proj["k"], c.done)
                if not c.first_ever:
                    act.wait_ge(k_turned, c.s)
                    act.wait_ge(lo_done["kT"], c.s)
                nc.scalar.activation(k32[:, :], A[:, :], ACT.Silu).then_inc(silu["k"], 1)
                act.wait_ge(silu["k"], c.done)
                if not c.first_ever:
                    act.wait_ge(scores_done, c.s)
                nc.scalar.copy(hi["kT"][:, :], k32[:, :]).then_inc(hi_done["kT"], 1)
                if not c.first_ever:
                    squares(Step(i, k - 1))
                act.wait_ge(proj["v"], c.done)
                if not c.first_ever:
                    act.wait_ge(v_turned, c.s)
                nc.scalar.activation(v32[:, :], B[:, :], ACT.Silu).then_inc(silu["v"], 1)
                if not c.first_ever:
                    o_high(Step(i, k - 1))
                act.wait_ge(proj["q"], c.done)
                if not c.first_ever:
                    act.wait_ge(lo_done["q"], c.s)
                    act.wait_ge(qd_done, c.s)
                nc.scalar.activation(q32[:, :], A[:, :], ACT.Silu).then_inc(silu["q"], 1)
                act.wait_ge(silu["q"], c.done)
                nc.scalar.copy(hi["q"][:, :], q32[:, :]).then_inc(hi_done["q"], 1)
                wait_apart(act, k_turned, c.done)
                if not c.first_ever:
                    act.wait_ge(kv_done, c.s)
                nc.scalar.activation(hi["k"][:, :], TK[:, :], ACT.Copy, scale=kdecay(c)).then_inc(hi_done["k"], 1)
                act.wait_ge(v_turned, c.done)
                nc.scalar.copy(hi["v"][:, :], TV[:, :]).then_inc(hi_done["v"], 1)
                act.wait_ge(st_masked, c.done)
                nc.scalar.copy(hi["st"][:, :], st32[:, :]).then_inc(hi_done["st"], 1)
                act.wait_ge(states, SCANS * c.seq + (SCANS if c.second else BT))
                to, from_ = state_parts(c)
                nc.scalar.copy(hi["s"][:, to * P:].rearrange("p (c n) -> p c n", n=P),
                               state[:, from_:from_ + BT - to, :]).then_inc(hi_done["s"], 1)
                act.wait_ge(proj["g"], c.done)
                nc.scalar.activation(gate[:, :], B[:, :], ACT.Sigmoid).then_inc(gate_done, 1)

            for k in range(PEELED):
                slot(0, k)
            with act.Fori(0, HEADS - 1) as i:
                for k in range(PEELED, PEELED + BLOCKS):
                    slot(i, k)
            for k in range(PEELED, BLOCKS):
                slot(HEADS - 1, k)
            end = Step(HEADS - 1, BLOCKS - 1)
            squares(end)
            o_high(end)

            act.wait_ge(o_var_ready, 1)
            nc.scalar.activation(o_std[:, :], o_var[:, :], ACT.Sqrt).then_inc(o_std_ready, 1)
            off = TILES
            with act.Fori(0, TILES // 4) as i:
                for u in range(4):
                    root(4 * i + u, u)
                    if u:
                        part_of_xn(4 * i + u - 1, u - 1)
                part_of_xn(4 * i + 3, 3)

            def f_slot(i, k):
                c = Step(i, k)
                act.wait_ge(fg_proj, c.done)
                if not c.first_ever:
                    act.wait_ge(f_mul, c.s)
                nc.scalar.activation(gate[:, :], f_banks(c)[0][:, :], ACT.Silu).then_inc(f_silu, 1)
                act.wait_ge(f_mul, c.done)
                if c.first_ever:
                    act.wait_ge(y_done, BT * STEPS)
                else:
                    act.wait_ge(d_done, BT * c.s)
                nc.scalar.copy(hi["o"][:, :], o32[:, :]).then_inc(f_hi, 1)

            for k in range(PEELED):
                f_slot(0, k)
            with act.Fori(0, CHUNKS - 1) as i:
                for k in range(PEELED, PEELED + BLOCKS):
                    f_slot(i, k)
            for k in range(PEELED, BLOCKS):
                f_slot(CHUNKS - 1, k)

        @block.vector
        def _(dve):
            def normalise(t, u):
                b = u % 2
                ops = LN_OPS * (off + t)

                def col(x):
                    return x[:, b:b + 1]

                wait_apart(dve, h_ready, off + t + 1)
                nc.vector.bn_stats(stats[:, b, :], acc_tile(t)).then_inc(ln_op, 1)
                wait_apart(dve, ln_op, ops + 1)
                nc.vector.bn_aggr(mv[:, b, :], stats[:, b, :]).then_inc(ln_op, 1)
                dve.wait_ge(ln_op, ops + 2)
                nc.vector.tensor_scalar(col(var), mv[:, b, 1:2], LN_EPS, None, ALU.add).then_inc(var_ready, 1)
                if u:
                    low_of_xn(t - 1, u - 1)
                dve.wait_ge(std_ready, off + t + 1)
                nc.vector.reciprocal(col(rstd0), col(std)).then_inc(ln_op, 1)
                dve.wait_ge(ln_op, ops + 3)
                nc.vector.tensor_tensor(col(newton), col(rstd0), col(rstd0), ALU.mult).then_inc(ln_op, 1)
                dve.wait_ge(ln_op, ops + 4)
                nc.vector.tensor_tensor(col(std), col(newton), col(var), ALU.mult).then_inc(ln_op, 1)
                dve.wait_ge(ln_op, ops + 5)
                nc.vector.tensor_scalar(col(newton), col(std), -0.5, 1.5, ALU.mult, ALU.add).then_inc(ln_op, 1)
                dve.wait_ge(ln_op, ops + 6)
                nc.vector.tensor_tensor(col(rstd), col(rstd0), col(newton), ALU.mult).then_inc(ln_op, 1)
                dve.wait_ge(ln_op, ops + 7)
                nc.vector.tensor_scalar(xn[b][:, :], acc_tile(t), mv[:, b, 0:1], col(rstd),
                                        ALU.subtract, ALU.mult).then_inc(xn_ready, 1)
                nc.vector.engine_nop().then_inc(ln_op, 1)

            def low_of_xn(t, u):
                cols = bass.ds(P * t, P)
                dve.wait_ge(xn_hi_done, off + t + 1)
                nc.vector.tensor_tensor(xn_lo[:, :, cols], four((ST, KV)[u % 2]), xn_hi[:, :, cols].bitcast(F32),
                                        ALU.subtract).then_inc(xn_lo_done, 1)

            off = 0
            with dve.Fori(0, TILES // 4) as i:
                for u in range(4):
                    t = 4 * i + u
                    dve.wait_ge(delta_done, t + 1)
                    nc.vector.scalar_tensor_tensor(acc_tile(t), (TK, TV)[u % 2][:, :], SCALING, acc_tile(t),
                                                   ALU.mult, ALU.add).then_inc(h_ready, 1)
                    normalise(t, u)
                low_of_xn(4 * i + 3, 3)

            def gate_output(p):
                dve.wait_ge(o_done, p.done)
                dve.wait_ge(gate_done, p.done)
                if not p.first_ever:
                    dve.wait_ge(hi_done["o"], p.s)
                nc.vector.scalar_tensor_tensor(o32[:, :], O[:, :], column(normw, p.head), gate[:, :],
                                               ALU.mult, ALU.mult).then_inc(o_gated, 1)

            def low(n, count, from_):
                dve.wait_ge(hi_done[n], count)
                nc.vector.tensor_tensor(lo[n][:, :], from_, hi[n][:, :].bitcast(F32),
                                        ALU.subtract).then_inc(lo_done[n], 1)

            def add_projection(p):
                for c in range(BT):
                    t = BT * p.tc + c
                    dve.wait_ge(y_done, BT * p.s + c + 1)
                    nc.vector.tensor_tensor(acc[:, t, :], y_bank[c][:, :], acc[:, t, :], ALU.add
                                            ).then_inc(y_added, 1)

            def slot(i, k):
                c = Step(i, k)
                if not c.first_ever:
                    gate_output(Step(i, k - 1))
                low("kT", c.done, k32[:, :])
                if not c.first_ever:
                    low("o", c.s, o32[:, :])
                low("q", c.done, q32[:, :])
                dve.wait_ge(hi_done["k"], c.done)
                nc.vector.scalar_tensor_tensor(lo["k"][:, :], TK[:, :], kdecay(c), hi["k"][:, :].bitcast(F32),
                                               ALU.mult, ALU.subtract).then_inc(lo_done["k"], 1)
                low("v", c.done, TV[:, :])
                if not c.first_ever:
                    add_projection(Step(i, k - 1))
                dve.wait_ge(scores_done, c.done)
                if not c.first_ever:
                    dve.wait_ge(hi_done["st"], c.s)
                decay = tab[:, bass.ds(c.head, 1), 0:P].broadcast_to([P, BT, P])
                nc.vector.tensor_tensor(four(st32), four(ST), decay, ALU.mult).then_inc(st_masked, 1)
                dve.wait_ge(kv_done, c.done)
                if not c.first_ever:
                    dve.wait_ge(hi_done["s"], c.s)
                for n in range(SCANS - BT if c.second else BT):
                    at = n + (BT if c.second else 0)
                    if at == 0:
                        nc.vector.tensor_copy(state[:, 1, :], tile(KV, 0)).then_inc(states, 1)
                    else:
                        dve.wait_ge(states, SCANS * c.seq + at)
                        nc.vector.scalar_tensor_tensor(state[:, at + 1, :], state[:, at, :], cdecay(c), tile(KV, n),
                                                       ALU.mult, ALU.add).then_inc(states, 1)
                low("st", c.done, st32[:, :])
                dve.wait_ge(hi_done["s"], c.done)
                to, from_ = state_parts(c)
                part = slice(to * P, BLOCK)
                nc.vector.tensor_tensor(lo["s"][:, part].rearrange("p (c n) -> p c n", n=P),
                                        state[:, from_:from_ + BT - to, :],
                                        hi["s"][:, part].bitcast(F32).rearrange("p (c n) -> p c n", n=P),
                                        ALU.subtract).then_inc(lo_done["s"], 1)

            dve.wait_ge(masked, 1)
            slot(0, 0)
            dve.wait_ge(acc_zero, TILES)
            for k in range(1, PEELED):
                slot(0, k)
            with dve.Fori(0, HEADS - 1) as i:
                for k in range(PEELED, PEELED + BLOCKS):
                    slot(i, k)
            for k in range(PEELED, BLOCKS):
                slot(HEADS - 1, k)
            end = Step(HEADS - 1, BLOCKS - 1)
            gate_output(end)
            low("o", end.done, o32[:, :])
            add_projection(end)

            dve.wait_ge(ss_summed, 1)
            nc.vector.tensor_scalar(o_var[:, :], A[:, 0:2 * TILES].rearrange("p (t a) -> p t a", a=2)[:, :, 0],
                                    1.0 / INNER, RMS_EPS, ALU.mult, ALU.add).then_inc(o_var_ready, 1)
            dve.wait_ge(o_std_ready, 1)
            nc.vector.reciprocal(o_r0[:, :], o_std[:, :]).then_inc(o_rms_op, 1)
            dve.wait_ge(o_rms_op, 1)
            nc.vector.tensor_tensor(o_newton[:, :], o_r0[:, :], o_r0[:, :], ALU.mult).then_inc(o_rms_op, 1)
            dve.wait_ge(o_rms_op, 2)
            nc.vector.tensor_tensor(o_std[:, :], o_newton[:, :], o_var[:, :], ALU.mult).then_inc(o_rms_op, 1)
            dve.wait_ge(o_rms_op, 3)
            nc.vector.tensor_scalar(o_newton[:, :], o_std[:, :], -0.5, 1.5, ALU.mult, ALU.add).then_inc(o_rms_op, 1)
            dve.wait_ge(o_rms_op, 4)
            nc.vector.tensor_tensor(o_r[:, :], o_r0[:, :], o_newton[:, :], ALU.mult).then_inc(o_rms_op, 1)
            dve.wait_ge(o_rms_op, 5)
            dve.wait_ge(v_turned, STEPS)
            off = TILES
            with dve.Fori(0, TILES // 4) as i:
                for u in range(4):
                    t = 4 * i + u
                    dve.wait_ge(h_back[u % 2], DMA * (2 * i + u // 2 + 1))
                    nc.vector.scalar_tensor_tensor(acc_tile(t), acc_tile(t), column(o_r, t), h_in[u % 2][:, :],
                                                   ALU.mult, ALU.add).then_inc(h_ready, 1)
                    normalise(t, u)
                low_of_xn(4 * i + 3, 3)

            nc.vector.engine_nop().then_inc(d_free, BT)

            def add_down(p):
                for c in range(BT):
                    t = BT * p.tc + c
                    dve.wait_ge(d_done, BT * p.s + c + 1)
                    nc.vector.tensor_tensor(acc[:, t, :], y_bank[c][:, :], acc[:, t, :], ALU.add
                                            ).then_inc(d_free, 1)

            def f_slot(i, k):
                c = Step(i, k)
                dve.wait_ge(fu_proj, c.done)
                dve.wait_ge(f_silu, c.done)
                if c.first_ever:
                    dve.wait_ge(hi_done["o"], STEPS)
                else:
                    dve.wait_ge(f_lo, c.s)
                nc.vector.tensor_tensor(o32[:, :], f_banks(c)[1][:, :], gate[:, :], ALU.mult).then_inc(f_mul, 1)
                if not c.first_ever:
                    add_down(Step(i, k - 1))
                dve.wait_ge(f_hi, c.done)
                nc.vector.tensor_tensor(lo["o"][:, :], o32[:, :], hi["o"][:, :].bitcast(F32),
                                        ALU.subtract).then_inc(f_lo, 1)

            for k in range(PEELED):
                f_slot(0, k)
            with dve.Fori(0, CHUNKS - 1) as i:
                for k in range(PEELED, PEELED + BLOCKS):
                    f_slot(i, k)
            for k in range(PEELED, BLOCKS):
                f_slot(CHUNKS - 1, k)
            add_down(Step(CHUNKS - 1, BLOCKS - 1))

        def product(to, w, w_at, x, x_at, start, stop):
            nc.tensor.matmul(to, w[0][w_at], x[0][x_at], start=start, stop=False)
            nc.tensor.matmul(to, w[0][w_at], x[1][x_at], start=False, stop=False)
            return nc.tensor.matmul(to, w[1][w_at], x[0][x_at], start=False, stop=stop)

        def at(c):
            return (slice(None), slice(c * P, (c + 1) * P))

        def project(to, n, tc):
            for kc in range(KC):
                last = product(to[:, :], (w_hi[n], w_lo[n]), at(kc), (xn_hi, xn_lo),
                               (slice(None), kc, slice(tc * BLOCK, (tc + 1) * BLOCK)), kc == 0, kc == KC - 1)
            return last

        @block.tensor
        def _(pe):
            def turn_xn(t, u):
                pe.wait_ge(xn_ready, off + t + 1)
                for kc in range(KC):
                    last = nc.tensor.transpose(tile((ST, KV)[u % 2], kc), tile(xn[u % 2], kc), ident[:, :])
                last.then_inc(xn_turned, 1)

            off = 0
            pe.wait_ge(const_step, 3)
            with pe.Fori(0, TILES // 4) as i:
                for u in range(4):
                    t = 4 * i + u
                    pe.wait_ge(gathered[u], 2 * DMA * (i + 1))
                    nc.tensor.transpose((A, B)[u % 2][0:RANK, 0:P], a_tok[:, u, :], ident[:, :]
                                        ).then_inc(a_turned, 1)
                    pe.wait_ge(aT_ready, t + 1)
                    nc.tensor.matmul((TK, TV)[u % 2][:, :], aT[:, u % 2, :], loraB[0:RANK, :], start=True, stop=True
                                     ).then_inc(delta_done, 1)
                    if u:
                        turn_xn(t - 1, u - 1)
                turn_xn(4 * i + 3, 3)

            def output(p):
                pe.wait_ge(lo_done["st"], p.done)
                pe.wait_ge(lo_done["s"], p.done)
                pe.wait_ge(lo_done["qd"], p.done)
                first_state = state_parts(p)[0]
                for c in range(BT):
                    last = product(tile(O, c), (hi["v"], lo["v"]), at(c), (hi["st"], lo["st"]), at(c),
                                   True, c < first_state)
                    if c >= first_state:
                        last = product(tile(O, c), (hi["s"], lo["s"]), at(c), (hi["qd"], lo["qd"]), at(c),
                                       False, True)
                last.then_inc(o_done, 1)

            def project_out(p):
                if p.tc == 0:
                    pe.wait_ge(w_ready["o"], p.head + 1)
                pe.wait_ge(lo_done["o"], p.done)
                pe.wait_ge(st_masked, p.done)
                pe.wait_ge(states, SCANS * p.seq + (SCANS if p.second else BT))
                pe.wait_ge(sq_done, p.done)
                for c in range(BT):
                    product(y_bank[c][:, :], (hi["o"], lo["o"]), at(c), (w_hi["o"], w_lo["o"]),
                            (slice(None), slice(0, D)), True, True).then_inc(y_done, 1)

            def slot(i, k):
                c = Step(i, k)
                if c.tc == 0:
                    pe.wait_ge(w_ready["k"], c.head + 1)
                pe.wait_ge(xn_lo_done, BT * (c.tc + 1))
                if not c.first_ever:
                    pe.wait_ge(silu["q"], c.s)
                project(A, "k", c.tc).then_inc(proj["k"], 1)
                if not c.first_ever:
                    output(Step(i, k - 1))
                    pe.wait_ge(gate_done, c.s)
                if c.tc == 0:
                    pe.wait_ge(w_ready["v"], c.head + 1)
                project(B, "v", c.tc).then_inc(proj["v"], 1)
                pe.wait_ge(silu["k"], c.done)
                if c.tc == 0:
                    pe.wait_ge(w_ready["q"], c.head + 1)
                project(A, "q", c.tc).then_inc(proj["q"], 1)
                if not c.first_ever:
                    pe.wait_ge(lo_done["k"], c.s)
                for n in range(BT):
                    last = nc.tensor.transpose(tile(TK, n), tile(k32, n), ident[:, :])
                last.then_inc(k_turned, 1)
                pe.wait_ge(silu["v"], c.done)
                if not c.first_ever:
                    pe.wait_ge(lo_done["v"], c.s)
                for n in range(BT):
                    last = nc.tensor.transpose(tile(TV, n), tile(v32, n), ident[:, :])
                last.then_inc(v_turned, 1)
                if not c.first_ever:
                    project_out(Step(i, k - 1))
                pe.wait_ge(lo_done["kT"], c.done)
                pe.wait_ge(lo_done["q"], c.done)
                if not c.first_ever:
                    pe.wait_ge(y_added, BT * (c.s - 1) + 1)
                for n in range(BT):
                    last = product(tile(ST, n), (hi["kT"], lo["kT"]), at(n), (hi["q"], lo["q"]), at(n), True, True)
                last.then_inc(scores_done, 1)
                pe.wait_ge(lo_done["k"], c.done)
                pe.wait_ge(lo_done["v"], c.done)
                if not c.first_ever:
                    pe.wait_ge(y_added, BT * c.s)
                for n in range(SCANS - BT if c.second else BT):
                    last = product(tile(KV, n), (hi["k"], lo["k"]), at(n), (hi["v"], lo["v"]), at(n), True, True)
                last.then_inc(kv_done, 1)
                pe.wait_ge(silu["v"], c.done)
                if c.tc == 0:
                    pe.wait_ge(w_ready["g"], c.head + 1)
                project(B, "g", c.tc).then_inc(proj["g"], 1)

            for k in range(PEELED):
                slot(0, k)
            with pe.Fori(0, HEADS - 1) as i:
                for k in range(PEELED, PEELED + BLOCKS):
                    slot(i, k)
            for k in range(PEELED, BLOCKS):
                slot(HEADS - 1, k)
            end = Step(HEADS - 1, BLOCKS - 1)
            output(end)
            project_out(end)

            pe.wait_ge(ssq_added, STEPS)
            for t in range(TILES):
                last = nc.tensor.matmul(A[:, 2 * t:2 * t + 2], tile(ssq, t), ones2[:, :], start=True, stop=True)
            last.then_inc(ss_summed, 1)
            off = TILES
            with pe.Fori(0, TILES // 4) as i:
                for u in range(4):
                    turn_xn(4 * i + u, u)

            def f_down_product(p):
                if p.tc == 0:
                    pe.wait_ge(w_ready["o"], HEADS + p.head + 1)
                pe.wait_ge(f_lo, p.done)
                for c in range(BT):
                    pe.wait_ge(d_free, BT * p.s + c + 1)
                    product(y_bank[c][:, :], (hi["o"], lo["o"]), at(c), (w_hi["o"], w_lo["o"]),
                            (slice(None), slice(0, D)), True, True).then_inc(d_done, 1)

            def f_slot(i, k):
                c = Step(i, k)
                if c.tc == 0:
                    pe.wait_ge(w_ready["k"], HEADS + c.head + 1)
                pe.wait_ge(xn_lo_done, TILES + BT * (c.tc + 1))
                if c.later:
                    pe.wait_ge(f_mul, c.s - 1)
                project(f_banks(c)[0], "k", c.tc).then_inc(fg_proj, 1)
                if c.tc == 0:
                    pe.wait_ge(w_ready["v"], HEADS + c.head + 1)
                project(f_banks(c)[1], "v", c.tc).then_inc(fu_proj, 1)
                if not c.first_ever:
                    f_down_product(Step(i, k - 1))

            for k in range(PEELED):
                f_slot(0, k)
            with pe.Fori(0, CHUNKS - 1) as i:
                for k in range(PEELED, PEELED + BLOCKS):
                    f_slot(i, k)
            for k in range(PEELED, BLOCKS):
                f_slot(CHUNKS - 1, k)
            f_down_product(Step(CHUNKS - 1, BLOCKS - 1))


def kernel(x, L0_tok_W, L0_tok_lora_A, L0_tok_lora_B, L0_attn_slope_rate, L0_attn_w_qkv, L0_attn_w_gate,
           L0_attn_w_out, L0_attn_norm_w, L0_ffn_w_gate, L0_ffn_w_up, L0_ffn_w_down):
    import concourse.bacc as bacc
    from concourse.bass_utils import run_bass_kernel_spmd

    def by_input(w):
        w = np.asarray(w)
        n = w.shape[0] // P
        return w.reshape(n, P, KC, P).transpose(0, 3, 2, 1).reshape(n, P, KC * P)

    qkv = by_input(L0_attn_w_qkv)
    arrays = {
        "ids": np.asarray(x).reshape(TILES, P).T,
        "table": np.asarray(L0_tok_W),
        "lora_a": np.asarray(L0_tok_lora_A).T,
        "lora_b": np.asarray(L0_tok_lora_B).T,
        "slopes": np.asarray(L0_attn_slope_rate).reshape(1, HEADS),
        "norm_w": np.asarray(L0_attn_norm_w).reshape(HEADS, P).T,
        "w_qkv": qkv.reshape(HEADS, 3, P, D).transpose(1, 0, 2, 3),
        "w_gate": by_input(L0_attn_w_gate),
        "w_out": np.asarray(L0_attn_w_out).T.reshape(HEADS, P, D),
        "f_gate": by_input(L0_ffn_w_gate),
        "f_up": by_input(L0_ffn_w_up),
        "f_down": np.asarray(L0_ffn_w_down).T.reshape(CHUNKS, P, D),
    }
    arrays = {n: np.ascontiguousarray(a) for n, a in arrays.items()}
    nc = bacc.Bacc("TRN2", target_bir_lowering=False, num_devices=1)
    args = [nc.dram_tensor(n, a.shape, mybir.dt.from_np(a.dtype), kind="ExternalInput").ap()
            for n, a in arrays.items()]
    h_spill = nc.dram_tensor("h_spill", (TILES, P, D), F32, kind="Internal").ap()
    out = nc.dram_tensor("out", (T, D), F32, kind="ExternalOutput").ap()
    build(nc, *args, h_spill, out)
    r = run_bass_kernel_spmd(nc, [arrays], core_ids=[0])
    return r.results[0]["out"].reshape(2, T // 2, D)
```

```python
from contextlib import ExitStack

import numpy as np
import concourse.bass as bass
from concourse import mybir
from concourse.alu_op_type import AluOpType as ALU

F32 = mybir.dt.float32
F32R = mybir.dt.float32r
I32 = mybir.dt.int32
ACT = mybir.ActivationFunctionType

P = 128
D = 512
KC = D // P
T = 2048
TILES = T // P
BLOCK = 512
BT = BLOCK // P
BLOCKS = T // BLOCK
SEQ_TILES = 1024 // P
HEADS = 16
INNER = HEADS * P
CHUNKS = 2048 // P
RANK = 16
PARTS = 96
SCALING = 32.0 / RANK
LN_EPS = 1e-5
RMS_EPS = 1e-6
STEPS = HEADS * BLOCKS
F_STEPS = CHUNKS * BLOCKS
PEELED = BLOCKS - 1
LAST_HEADS = 2
SCANS = SEQ_TILES - 1
ROOT_OPS = 2 + 3 * 3
ROOT_MAGIC = 0x5F3759DF
LN_OPS = 2 * BT + ROOT_OPS + 2
RMS_OPS = ROOT_OPS
TAB = 2 * P + 1
DMA = 16


class Step:

    def __init__(self, i, k):
        self.s = BLOCKS * i + k
        self.done = self.s + 1
        self.tc = k % BLOCKS
        self.head = i + k // BLOCKS
        self.second = self.tc % 2
        self.seq = 2 * self.head + self.tc // 2
        self.states = SCANS * self.seq + (SCANS if self.second else BT)
        static = isinstance(self.s, int)
        self.first_ever = static and self.s == 0
        self.later = not static or self.s > 1
        self.last_head = static and self.head == HEADS - 1


def build(nc, ids, table, lora_a, lora_b, slopes, norm_w, w_qkv, w_gate, w_out, f_gate, f_up, f_down, out):
    with ExitStack() as ctx:
        def sb(name, shape, dt=F32):
            return ctx.enter_context(nc.sbuf_tensor(name, shape, dt))

        def sem(name):
            return ctx.enter_context(nc.semaphore(name))

        h = sb("h", [P, TILES, D])
        acc = sb("acc", [P, TILES, D])
        xn_hi = sb("xn_hi", [P, KC, T], F32R)
        xn_lo = sb("xn_lo", [P, KC, T], F32R)
        ssq = sb("ssq", [P, T])
        slope = sb("slope", [P, HEADS])
        normw = sb("normw", [P, HEADS])
        ident = sb("ident", [P, P])
        ones2 = sb("ones2", [P, 2])
        raw_pair = [sb(f"raw{n}", [P, D]) for n in range(3)]
        raw = {"k": raw_pair[0], "v": raw_pair[1], "q": raw_pair[0], "g": raw_pair[1], "o": raw_pair[2]}
        w_hi = {n: sb(f"{n}_whi", [P, D], F32R) for n in "kvqgo"}
        w_lo = {n: sb(f"{n}_wlo", [P, D], F32R) for n in "kvqgo"}
        exponent = sb("exponent", [P, TAB])
        tab = sb("tab", [P, TAB])
        decay_qk, decay_q, decay_k, decay_chunk = tab[:, 0:P], tab[:, P:2 * P], tab[:, 2 * P:TAB], tab[:, 2 * P - 1:2 * P]
        k, v, q, q_dec, k_tok, v_tok, scores, o, gate, sq = (
            sb(n, [P, BLOCK]) for n in ("k", "v", "q", "q_dec", "k_tok", "v_tok", "scores", "o", "gate", "sq"))
        o_hi, o_lo = sb("o_hi", [P, BLOCK], F32R), sb("o_lo", [P, BLOCK], F32R)
        state = sb("state", [P, SEQ_TILES, P])
        idx = sb("idx", [P, TILES], I32)
        a_tok = sb("a_tok", [P, TILES, RANK])
        a_parts = sb("a_parts", [P, TILES, PARTS], F32R)
        stats = sb("stats", [P, BT, 6])
        mv = sb("mv", [P, BT, 2])
        var, newton, rstd, shift = (sb(n, [P, BT]) for n in ("var", "newton", "rstd", "shift"))
        o_var, o_newton, o_r = (sb(n, [P, BT]) for n in ("o_var", "o_newton", "o_r"))
        aT = sb("aT", [PARTS, BLOCK], F32R)
        loraB = sb("loraB", [PARTS, D], F32R)
        b_raw = scores[0:PARTS, :]
        exponent_i = acc[:, TILES - 2, 0:TAB].bitcast(I32)

        A, B, TK, TV, ST, KV, O, Y3 = (
            ctx.enter_context(nc.psum_tensor(f"bank_{n}", [P, BLOCK], F32))
            for n in ("a", "b", "tk", "tv", "st", "kv", "o", "y3"))
        y_bank = (ST, KV, O, Y3)

        idx_in, consts_in, const_step, exponents, tab_exp, tab_ready, acc_zero, ssq_zero = (
            sem(n) for n in ("idx_in", "consts_in", "const_step", "exponents",
                             "tab_exp", "tab_ready",
                             "acc_zero",
                             "ssq_zero"))
        a_gathered = [sem(f"a_gathered{b}") for b in range(BLOCKS)]
        gathered = [sem(f"gathered{t}") for t in range(TILES)]
        b_zeroed, b_in, b_hi_done, b_ready = (sem(n) for n in ("b_zeroed", "b_in", "b_hi_done", "b_ready"))
        a_zeroed = sem("a_zeroed")
        a_hi_done, a_parts_done = sem("a_hi_done"), sem("a_parts_done")
        a_turned, aT_ready = sem("a_turned"), sem("aT_ready")
        delta_done, h_ready, xn_ready = sem("delta_done"), sem("h_ready"), sem("xn_ready")
        ln_op = sem("ln_op")
        xn_turned, xn_hi_done, xn_lo_done = (
            sem(n) for n in ("xn_turned", "xn_hi_done", "xn_lo_done"))
        ss_summed, o_var_ready = sem("ss_summed"), sem("o_var_ready")
        rms_op = sem("rms_op")

        loaded = {n: sem(f"loaded_{n}") for n in "kvqgo"}
        w_hi_done = {n: sem(f"w_hi_done_{n}") for n in "kvqgo"}
        w_ready = {n: sem(f"w_ready_{n}") for n in "kvqgo"}

        proj = {n: sem(f"proj_{n}") for n in "kvqg"}
        silu = {n: sem(f"silu_{n}") for n in "kvq"}
        k_turned, v_turned, k_tok_done, v_tok_done, q_dec_done = (
            sem(n) for n in ("k_turned", "v_turned", "k_tok_done", "v_tok_done", "q_dec_done"))
        scored, masked, kv_done, states = (
            sem(n) for n in ("scored", "masked", "kv_done",
                             "states"))
        o_done, gate_done, o_gated, sq_done, ssq_added, o_hi_done, o_lo_done = (
            sem(n) for n in ("o_done", "gate_done", "o_gated", "sq_done", "ssq_added", "o_hi_done", "o_lo_done"))
        y_done, y_added = sem("y_done"), sem("y_added")
        fg_proj, fu_proj, f_silu, f_mul, f_hi, f_lo = (
            sem(n) for n in ("fg_proj", "fu_proj", "f_silu", "f_mul", "f_hi", "f_lo"))
        d_done, d_added, out_done = sem("d_done"), sem("d_added"), sem("out_done")

        block = ctx.enter_context(nc.Block())

        def wait_apart(eng, semaphore, count, least=1):
            if not isinstance(count, int):
                eng.lower_val(count)
                eng.wait_ge(semaphore, least)
            eng.wait_ge(semaphore, count)

        def tile(ap, c):
            return ap[:, c * P:(c + 1) * P]

        def four(ap):
            return ap[:, :].rearrange("p (c n) -> p c n", c=BT)

        def for_each_tile(ap):
            return ap.unsqueeze(1).broadcast_to([P, BT, P])

        def column(t, c):
            return t[:, bass.ds(c, 1)]

        def first_state(c):
            return 0 if c.second else 1

        def scans(c):
            return SCANS - BT if c.second else BT

        def f_banks(c):
            return (TK, TV) if c.tc % 2 else (A, B)

        turn_banks = (TV, TK, O, Y3)

        def f_turn_banks(n):
            return (O, Y3) + ((TK, TV) if n % 2 else (A, B))

        def ss_bank(b):
            return O if b == BLOCKS - 1 else TV

        attn_src = {"q": lambda n: w_qkv[0, n], "k": lambda n: w_qkv[1, n], "v": lambda n: w_qkv[2, n],
                    "g": lambda n: w_gate[n], "o": lambda n: w_out[n]}
        ffn_src = {"k": lambda n: f_gate[n], "v": lambda n: f_up[n], "o": lambda n: f_down[n]}
        former = {"k": ("q", 0), "v": ("g", 0), "q": ("k", 1), "g": ("v", 1), "o": ("o", 0)}

        @block.sync
        def _(sp):
            sp.dma_start(idx[:, :], ids).then_inc(idx_in, DMA)
            sp.wait_ge(b_zeroed, 1)
            for row in range(0, PARTS, 32):
                sp.dma_start(b_raw[row:row + RANK, :], lora_b).then_inc(b_in, DMA)
            sp.dma_start(slope[:, :], slopes.broadcast_to([P, HEADS])).then_inc(consts_in, DMA)
            sp.dma_start(normw[:, :], norm_w).then_inc(consts_in, DMA)
            for n in "kvqgo":
                if former[n][1]:
                    sp.wait_ge(w_ready[former[n][0]], 1)
                sp.dma_start(raw[n][:, :], attn_src[n](0)).then_inc(loaded[n], DMA)
            with sp.Fori(1, HEADS) as i:
                for n in "kvqgo":
                    was, same = former[n]
                    wait_apart(sp, w_ready[was], i + same)
                    sp.dma_start(raw[n][:, :], attn_src[n](bass.ds(i, 1)).rearrange("a p n -> (a p) n")
                                 ).then_inc(loaded[n], DMA)
            for n in "kvo":
                sp.wait_ge(w_ready[former[n][0]], HEADS)
                sp.dma_start(raw[n][:, :], ffn_src[n](0)).then_inc(loaded[n], DMA)
            with sp.Fori(1, CHUNKS) as j:
                for n in "kvo":
                    wait_apart(sp, w_ready[n], HEADS + j)
                    sp.dma_start(raw[n][:, :], ffn_src[n](bass.ds(j, 1)).rearrange("a p n -> (a p) n")
                                 ).then_inc(loaded[n], DMA)
            for t in range(TILES):
                sp.wait_ge(d_added, BT * F_STEPS - TILES + t + 1)
                sp.dma_start(out[t * P:(t + 1) * P, :], h[:, t, :]).then_inc(out_done, DMA)
            sp.wait_ge(out_done, DMA * TILES)

        @block.gpsimd
        def _(pool):
            nc.gpsimd.memset(b_raw, 0.0).then_inc(b_zeroed, 1)
            nc.gpsimd.memset(a_parts[:, :, :].bitcast(F32), 0.0).then_inc(a_zeroed, 1)
            nc.gpsimd.iota(exponent_i[:, 0:P], pattern=[[-1, P]], base=0, channel_multiplier=1
                           ).then_inc(exponents, 1)
            nc.gpsimd.iota(exponent_i[:, P:2 * P], pattern=[[-1, P]], base=-1, channel_multiplier=0
                           ).then_inc(exponents, 1)
            nc.gpsimd.iota(exponent_i[:, 2 * P:TAB], pattern=[[1, 1]], base=1 - P, channel_multiplier=1
                           ).then_inc(exponents, 1)
            nc.gpsimd.memset(ident[:, :], 0.0).then_inc(const_step, 1)
            nc.gpsimd.memset(ones2[:, :], 1.0).then_inc(const_step, 1)

            def gather(b):
                tiles = range(BT * b, BT * (b + 1))
                row_of = {t: bass.IndirectOffsetOnAxis(idx[:, t:t + 1], 0) for t in tiles}
                for t in tiles:
                    nc.gpsimd.indirect_dma_start(a_tok[:, t, :], None, lora_a[:, :], row_of[t]
                                                 ).then_inc(a_gathered[b], DMA)
                for t in tiles:
                    nc.gpsimd.indirect_dma_start(h[:, t, :], None, table[:, :], row_of[t]
                                                 ).then_inc(gathered[t], DMA)

            def mask_table(c):
                wait_apart(pool, tab_exp, c.head + 1)
                nc.gpsimd.affine_select(out=decay_qk, in_=decay_qk, compare_op=ALU.is_ge, fill=0.0, base=0,
                                        pattern=[[1, P]], channel_multiplier=-1).then_inc(tab_ready, 1)

            pool.wait_ge(const_step, 2)
            nc.gpsimd.affine_select(out=ident[:, :], in_=ident[:, :], compare_op=ALU.not_equal, fill=1.0, base=0,
                                    pattern=[[-1, P]], channel_multiplier=1).then_inc(const_step, 1)
            pool.wait_ge(idx_in, DMA)
            gather(0)
            pool.wait_ge(exponents, 3)
            nc.gpsimd.tensor_scalar(exponent[:, :], exponent_i, 0.0, None, ALU.min).then_inc(exponents, 1)
            mask_table(Step(0, 0))
            for b in range(1, BLOCKS):
                gather(b)
            nc.gpsimd.memset(ssq[:, :], 0.0).then_inc(ssq_zero, 1)

            def zero_acc(b):
                pool.wait_ge(xn_turned, KC * (b + 1))
                nc.gpsimd.memset(acc[:, BT * b:BT * (b + 1), :], 0.0).then_inc(acc_zero, 1)

            def add_squares(p):
                cols = ssq[:, p.tc * BLOCK:(p.tc + 1) * BLOCK]
                pool.wait_ge(sq_done, p.done)
                nc.gpsimd.tensor_tensor(cols, cols, sq[:, :], ALU.add).then_inc(ssq_added, 1)

            def split_low(n, count):
                pool.wait_ge(w_hi_done[n], count)
                nc.gpsimd.tensor_tensor(w_lo[n][:, :], raw[n][:, :], w_hi[n][:, :].bitcast(F32),
                                        ALU.subtract).then_inc(w_ready[n], 1)

            def slot(i, kk):
                c = Step(i, kk)
                if c.tc == 0 and not c.first_ever:
                    mask_table(c)
                if not c.first_ever:
                    add_squares(Step(i, kk - 1))
                if c.tc == BLOCKS - 1:
                    for n in "kv":
                        split_low(n, c.head + 2)
                pool.wait_ge(silu["q"], c.done)
                nc.gpsimd.tensor_tensor(four(q_dec), four(q), for_each_tile(decay_q), ALU.mult
                                        ).then_inc(q_dec_done, 1)
                if c.tc == BLOCKS - 1 and not c.last_head:
                    for n in "qg":
                        split_low(n, c.head + 2)
                if c.tc == 0 and not c.first_ever:
                    split_low("o", c.head + 1)

            zero_acc(0)
            pool.wait_ge(ssq_zero, 1)
            for kk in range(PEELED):
                slot(0, kk)
                zero_acc(kk + 1)
            with pool.Fori(0, HEADS - LAST_HEADS) as i:
                for kk in range(PEELED, PEELED + BLOCKS):
                    slot(i, kk)
            for kk in range(PEELED, LAST_HEADS * BLOCKS):
                slot(HEADS - LAST_HEADS, kk)
            add_squares(Step(HEADS - 1, BLOCKS - 1))
            split_low("o", HEADS + 1)
            with pool.Fori(1, CHUNKS) as j:
                for n in "kvo":
                    split_low(n, HEADS + j + 1)

        @block.scalar
        def _(act):
            def decay_table(c):
                act_waits = (("states", states, SCANS * c.seq), ("masked", masked, c.s), ("q_dec", q_dec_done, c.s))
                if not c.first_ever:
                    for _, used, count in act_waits:
                        wait_apart(act, used, count)
                nc.scalar.activation(tab[:, :], exponent[:, :], ACT.Exp, scale=column(slope, c.head)
                                     ).then_inc(tab_exp, 1)

            def split_high(n, count):
                act.wait_ge(loaded[n], DMA * count)
                nc.scalar.copy(w_hi[n][:, :], raw[n][:, :]).then_inc(w_hi_done[n], 1)

            def normalise(n):
                act.wait_ge(ln_op, LN_OPS * (n + 1))
                for c in range(BT):
                    t = BT * (n % BLOCKS) + c
                    nc.scalar.activation(acc[:, t, :], h[:, t, :], ACT.Identity, scale=rstd[:, c:c + 1],
                                         bias=shift[:, c:c + 1]).then_inc(xn_ready, 1)

            def xn_high(n, banks):
                b = n % BLOCKS
                for kc in range(KC):
                    act.wait_ge(xn_turned, KC * n + kc + 1)
                    nc.scalar.copy(xn_hi[:, kc, b * BLOCK:(b + 1) * BLOCK], banks[kc][:, :]).then_inc(xn_hi_done, 1)

            def squares(p):
                act.wait_ge(o_gated, p.done)
                if not p.first_ever:
                    act.wait_ge(ssq_added, p.s)
                nc.scalar.activation(sq[:, :], O[:, :], ACT.Square).then_inc(sq_done, 1)

            def o_high(p):
                if not p.first_ever:
                    act.wait_ge(y_done, BT * p.s)
                nc.scalar.copy(o_hi[:, :], o[:, :]).then_inc(o_hi_done, 1)

            def keep_lora_rows(b):
                act.wait_ge(a_turned, b + 1)
                if b:
                    act.wait_ge(delta_done, BT * b)
                nc.scalar.copy(aT[:, :], TV[0:PARTS, :]).then_inc(aT_ready, 1)

            def lora_high(b):
                act.wait_ge(a_gathered[b], BT * DMA)
                act.wait_ge(a_zeroed, 1)
                for col in (0, 32):
                    nc.scalar.copy(a_parts[:, BT * b:BT * (b + 1), col:col + RANK], a_tok[:, BT * b:BT * (b + 1), :]
                                   ).then_inc(a_hi_done, 1)

            act.wait_ge(b_in, 3 * DMA)
            nc.scalar.copy(loraB[:, :], b_raw).then_inc(b_hi_done, 1)
            for n in "kv":
                split_high(n, 1)
            lora_high(0)
            keep_lora_rows(0)
            act.wait_ge(exponents, 4)
            act.wait_ge(consts_in, 2 * DMA)
            decay_table(Step(0, 0))
            for n in "qgo":
                split_high(n, 1)
            lora_high(1)
            normalise(0)
            xn_high(0, turn_banks)

            def slot(i, kk, ln=None):
                c = Step(i, kk)
                if ln is not None and ln < BLOCKS:
                    keep_lora_rows(ln)
                act.wait_ge(proj["k"], c.done)
                if not c.first_ever:
                    act.wait_ge(scored, c.s)
                nc.scalar.activation(k[:, :], A[:, :], ACT.Silu).then_inc(silu["k"], 1)
                if c.tc == 0 and not c.first_ever:
                    decay_table(c)
                act.wait_ge(proj["v"], c.done)
                nc.scalar.activation(v[:, :], B[:, :], ACT.Silu).then_inc(silu["v"], 1)
                if not c.first_ever:
                    squares(Step(i, kk - 1))
                    o_high(Step(i, kk - 1))
                act.wait_ge(k_turned, c.done)
                if not c.first_ever:
                    act.wait_ge(kv_done, c.s)
                if c.tc == 0:
                    act.wait_ge(tab_exp, c.head + 1)
                nc.scalar.activation(k_tok[:, :], TK[:, :], ACT.Copy, scale=decay_k).then_inc(k_tok_done, 1)
                act.wait_ge(v_turned, c.done)
                nc.scalar.copy(v_tok[:, :], TV[:, :]).then_inc(v_tok_done, 1)
                act.wait_ge(proj["q"], c.done)
                if not c.first_ever:
                    act.wait_ge(q_dec_done, c.s)
                nc.scalar.activation(q[:, :], A[:, :], ACT.Silu).then_inc(silu["q"], 1)
                if c.tc == BLOCKS - 1:
                    for n in "kv":
                        split_high(n, c.head + 2)
                if ln is not None:
                    if ln + 1 < BLOCKS:
                        lora_high(ln + 1)
                    normalise(ln)
                    xn_high(ln, turn_banks)
                act.wait_ge(proj["g"], c.done)
                nc.scalar.activation(gate[:, :], B[:, :], ACT.Sigmoid).then_inc(gate_done, 1)
                if c.tc == BLOCKS - 1 and not c.last_head:
                    for n in "qg":
                        split_high(n, c.head + 2)
                if c.tc == 0 and not c.first_ever:
                    act.wait_ge(y_done, BT * c.s)
                    split_high("o", c.head + 1)

            for kk in range(PEELED):
                slot(0, kk, ln=kk + 1)
            with act.Fori(0, HEADS - LAST_HEADS) as i:
                for kk in range(PEELED, PEELED + BLOCKS):
                    slot(i, kk)
            for kk in range(PEELED, LAST_HEADS * BLOCKS):
                early = kk - (LAST_HEADS * BLOCKS - 2)
                slot(HEADS - LAST_HEADS, kk, *((BLOCKS + early,) if early >= 0 else ()))
            end = Step(HEADS - 1, BLOCKS - 1)
            squares(end)
            o_high(end)

            def f_silu_of(c):
                act.wait_ge(fg_proj, c.done)
                if not c.first_ever:
                    act.wait_ge(f_mul, c.s)
                nc.scalar.activation(gate[:, :], f_banks(c)[0][:, :], ACT.Silu).then_inc(f_silu, 1)

            def f_high(c):
                act.wait_ge(f_mul, c.done)
                if c.first_ever:
                    act.wait_ge(y_done, BT * STEPS)
                else:
                    act.wait_ge(d_done, BT * c.s)
                nc.scalar.copy(o_hi[:, :], o[:, :]).then_inc(f_hi, 1)

            def f_slot(i, kk, norm=None, turned=None):
                c = Step(i, kk)
                f_silu_of(c)
                if norm is not None:
                    normalise(norm)
                if turned is not None:
                    xn_high(turned, f_turn_banks(turned))
                if c.tc == BLOCKS - 1 and not c.last_head:
                    split_high("k", HEADS + c.head + 2)
                f_high(c)
                if c.tc == 0:
                    split_high("o", HEADS + c.head + 1)
                if c.tc == BLOCKS - 1 and not c.last_head:
                    act.wait_ge(fu_proj, c.done)
                    split_high("v", HEADS + c.head + 2)

            f_slot(0, 0, norm=BLOCKS + 2)
            f_slot(0, 1, turned=BLOCKS + 2)
            f_slot(0, 2, norm=BLOCKS + 3, turned=BLOCKS + 3)
            with act.Fori(0, CHUNKS - 1) as i:
                for kk in range(PEELED, PEELED + BLOCKS):
                    f_slot(i, kk)
            f_slot(CHUNKS - 1, BLOCKS - 1)

        @block.vector
        def _(dve):
            def add_deltas(n, tiles=range(BT)):
                for c in tiles:
                    t = BT * n + c
                    dve.wait_ge(delta_done, t + 1)
                    dve.wait_ge(gathered[t], DMA)
                    nc.vector.scalar_tensor_tensor(h[:, t, :], (TK, TV)[c % 2][:, :], SCALING, h[:, t, :],
                                                   ALU.mult, ALU.add).then_inc(h_ready, 1)

            def inverse_root(y, tmp, x, op, ops):
                bits = tmp[:, :].bitcast(I32)
                nc.vector.tensor_scalar(bits, x[:, :].bitcast(I32), 1, None, ALU.logical_shift_right).then_inc(op, 1)
                dve.wait_ge(op, ops + 1)
                nc.vector.tensor_scalar(y[:, :].bitcast(I32), bits, -1.0, float(ROOT_MAGIC), ALU.mult, ALU.add
                                        ).then_inc(op, 1)
                for n in range(ops + 2, ops + ROOT_OPS, 3):
                    dve.wait_ge(op, n)
                    nc.vector.tensor_tensor(tmp[:, :], y[:, :], y[:, :], ALU.mult).then_inc(op, 1)
                    dve.wait_ge(op, n + 1)
                    nc.vector.scalar_tensor_tensor(tmp[:, :], tmp[:, :], -0.5, x[:, :], ALU.mult, ALU.mult
                                                   ).then_inc(op, 1)
                    dve.wait_ge(op, n + 2)
                    nc.vector.scalar_tensor_tensor(y[:, :], tmp[:, :], 1.5, y[:, :], ALU.add, ALU.mult
                                                   ).then_inc(op, 1)

            def scale_and_add(n):
                b, ops = n % BLOCKS, RMS_OPS * (n % BLOCKS)
                sums = ss_bank(b)[:, 0:2 * BT].rearrange("p (t a) -> p t a", a=2)[:, :, 0]
                dve.wait_ge(ss_summed, b + 1)
                nc.vector.tensor_scalar(o_var[:, :], sums, 1.0 / INNER, RMS_EPS, ALU.mult, ALU.add
                                        ).then_inc(o_var_ready, 1)
                dve.wait_ge(o_var_ready, b + 1)
                inverse_root(o_r, o_newton, o_var, rms_op, ops)
                dve.wait_ge(rms_op, ops + ROOT_OPS)
                for c in range(BT):
                    t = BT * b + c
                    nc.vector.scalar_tensor_tensor(h[:, t, :], acc[:, t, :], o_r[:, c:c + 1], h[:, t, :],
                                                   ALU.mult, ALU.add).then_inc(h_ready, 1)

            def statistics(n, tiles):
                for c in tiles:
                    dve.wait_ge(h_ready, BT * n + c + 1)
                    if n and not c:
                        dve.wait_ge(ln_op, LN_OPS * n)
                    nc.vector.bn_stats(stats[:, c, :], h[:, BT * (n % BLOCKS) + c, :]).then_inc(ln_op, 1)

            def scale_and_shift(n):
                ops = LN_OPS * n
                if n:
                    dve.wait_ge(xn_ready, BT * n)
                for c in range(BT):
                    dve.wait_ge(ln_op, ops + c + 1)
                    nc.vector.bn_aggr(mv[:, c, :], stats[:, c, :]).then_inc(ln_op, 1)
                ops += 2 * BT
                dve.wait_ge(ln_op, ops)
                nc.vector.tensor_scalar(var[:, :], mv[:, :, 1], LN_EPS, None, ALU.add).then_inc(ln_op, 1)
                dve.wait_ge(ln_op, ops + 1)
                inverse_root(rstd, newton, var, ln_op, ops + 1)
                dve.wait_ge(ln_op, ops + 1 + ROOT_OPS)
                nc.vector.scalar_tensor_tensor(shift[:, :], mv[:, :, 0], -1.0, rstd[:, :], ALU.mult, ALU.mult
                                               ).then_inc(ln_op, 1)

            def xn_low(n, banks):
                cols = slice((n % BLOCKS) * BLOCK, (n % BLOCKS + 1) * BLOCK)
                for kc in range(KC):
                    dve.wait_ge(xn_hi_done, KC * n + kc + 1)
                    nc.vector.tensor_tensor(xn_lo[:, kc, cols], banks[kc][:, :], xn_hi[:, kc, cols].bitcast(F32),
                                            ALU.subtract).then_inc(xn_lo_done, 1)

            def gate_output(p):
                dve.wait_ge(o_done, p.done)
                dve.wait_ge(gate_done, p.done)
                if not p.first_ever:
                    dve.wait_ge(o_hi_done, p.s)
                    dve.wait_ge(o_lo_done, p.s)
                nc.vector.scalar_tensor_tensor(o[:, :], O[:, :], column(normw, p.head), gate[:, :],
                                               ALU.mult, ALU.mult).then_inc(o_gated, 1)

            def o_low(p):
                dve.wait_ge(o_hi_done, p.done)
                nc.vector.tensor_tensor(o_lo[:, :], o[:, :], o_hi[:, :].bitcast(F32), ALU.subtract
                                        ).then_inc(o_lo_done, 1)

            def add_projection(p):
                for c in range(BT):
                    t = BT * p.tc + c
                    dve.wait_ge(y_done, BT * p.s + c + 1)
                    nc.vector.tensor_tensor(acc[:, t, :], y_bank[c][:, :], acc[:, t, :], ALU.add
                                            ).then_inc(y_added, 1)

            def slot(i, kk, ln=None):
                c = Step(i, kk)
                if ln is not None:
                    if ln < BLOCKS:
                        add_deltas(ln)
                    else:
                        scale_and_add(ln)
                if not c.first_ever:
                    gate_output(Step(i, kk - 1))
                if ln is not None:
                    statistics(ln, (0, 1))
                if not c.first_ever:
                    o_low(Step(i, kk - 1))
                if ln is not None:
                    statistics(ln, (2, 3))
                    scale_and_shift(ln)
                    if ln + 1 < BLOCKS:
                        lora_low(ln + 1)
                if not c.first_ever:
                    if isinstance(c.s, int) and c.s <= PEELED:
                        dve.wait_ge(acc_zero, c.s)
                    add_projection(Step(i, kk - 1))
                if ln is not None:
                    xn_low(ln, turn_banks)
                if c.tc == 0:
                    dve.wait_ge(tab_ready, c.head + 1)
                dve.wait_ge(scored, c.done)
                nc.vector.tensor_tensor(four(scores), four(ST), for_each_tile(decay_qk), ALU.mult
                                        ).then_inc(masked, 1)
                dve.wait_ge(kv_done, c.done)
                for n in range(scans(c)):
                    at = n + BT * c.second
                    if at == 0:
                        nc.vector.tensor_copy(state[:, 1, :], tile(KV, 0)).then_inc(states, 1)
                    else:
                        dve.wait_ge(states, SCANS * c.seq + at)
                        nc.vector.scalar_tensor_tensor(state[:, at + 1, :], state[:, at, :], decay_chunk,
                                                       tile(KV, n), ALU.mult, ALU.add).then_inc(states, 1)

            def split_low(n):
                dve.wait_ge(w_hi_done[n], 1)
                nc.vector.tensor_tensor(w_lo[n][:, :], raw[n][:, :], w_hi[n][:, :].bitcast(F32), ALU.subtract
                                        ).then_inc(w_ready[n], 1)

            def lora_low(b):
                tiles = slice(BT * b, BT * (b + 1))
                dve.wait_ge(a_hi_done, 2 * b + 1)
                nc.vector.tensor_tensor(a_parts[:, tiles, 64:64 + RANK], a_tok[:, tiles, :],
                                        a_parts[:, tiles, 0:RANK].bitcast(F32), ALU.subtract
                                        ).then_inc(a_parts_done, 1)

            dve.wait_ge(b_hi_done, 1)
            nc.vector.tensor_tensor(loraB[32:64, :], b_raw[32:64, :], loraB[32:64, :].bitcast(F32), ALU.subtract
                                    ).then_inc(b_ready, 1)
            for n in "kv":
                split_low(n)
            lora_low(0)
            for c in range(BT):
                add_deltas(0, (c,))
                statistics(0, (c,))
            scale_and_shift(0)
            for n in "qgo":
                split_low(n)
            lora_low(1)
            xn_low(0, turn_banks)
            for kk in range(PEELED):
                slot(0, kk, ln=kk + 1)
            dve.wait_ge(acc_zero, BLOCKS)
            with dve.Fori(0, HEADS - LAST_HEADS) as i:
                for kk in range(PEELED, PEELED + BLOCKS):
                    slot(i, kk)
            for kk in range(PEELED, LAST_HEADS * BLOCKS):
                early = kk - (LAST_HEADS * BLOCKS - 2)
                slot(HEADS - LAST_HEADS, kk, *((BLOCKS + early,) if early >= 0 else ()))
            end = Step(HEADS - 1, BLOCKS - 1)
            scale_and_add(BLOCKS + 2)
            gate_output(end)
            statistics(BLOCKS + 2, (0, 1))
            o_low(end)
            statistics(BLOCKS + 2, (2, 3))
            scale_and_shift(BLOCKS + 2)
            add_projection(end)

            def f_multiply(c):
                dve.wait_ge(fu_proj, c.done)
                dve.wait_ge(f_silu, c.done)
                if c.first_ever:
                    dve.wait_ge(o_hi_done, STEPS)
                else:
                    dve.wait_ge(f_hi, c.s)
                    dve.wait_ge(f_lo, c.s)
                nc.vector.tensor_tensor(o[:, :], f_banks(c)[1][:, :], gate[:, :], ALU.mult).then_inc(f_mul, 1)

            def f_low(c):
                dve.wait_ge(f_hi, c.done)
                nc.vector.tensor_tensor(o_lo[:, :], o[:, :], o_hi[:, :].bitcast(F32), ALU.subtract
                                        ).then_inc(f_lo, 1)

            def add_down(p):
                for c in range(BT):
                    t = BT * p.tc + c
                    dve.wait_ge(d_done, BT * p.s + c + 1)
                    nc.vector.tensor_tensor(h[:, t, :], y_bank[c][:, :], h[:, t, :], ALU.add).then_inc(d_added, 1)

            def f_slot(i, kk):
                f_multiply(Step(i, kk))
                add_down(Step(i, kk - 1))
                f_low(Step(i, kk))

            first, second, third = (Step(0, kk) for kk in range(PEELED))
            f_multiply(first)
            f_low(first)
            scale_and_add(BLOCKS + 3)
            f_multiply(second)
            xn_low(BLOCKS + 2, f_turn_banks(BLOCKS + 2))
            statistics(BLOCKS + 3, range(BT))
            scale_and_shift(BLOCKS + 3)
            add_down(first)
            f_low(second)
            f_multiply(third)
            xn_low(BLOCKS + 3, f_turn_banks(BLOCKS + 3))
            add_down(second)
            f_low(third)
            with dve.Fori(0, CHUNKS - 1) as i:
                for kk in range(PEELED, PEELED + BLOCKS):
                    f_slot(i, kk)
            f_slot(CHUNKS - 1, BLOCKS - 1)
            add_down(Step(CHUNKS - 1, BLOCKS - 1))

        def product(to, w, w_at, x, x_at, start, stop):
            nc.tensor.matmul(to, w[0][w_at], x[0][x_at], start=start, stop=False)
            nc.tensor.matmul(to, w[0][w_at], x[1][x_at], start=False, stop=False)
            return nc.tensor.matmul(to, w[1][w_at], x[0][x_at], start=False, stop=stop)

        def project(to, n, tc):
            cols = slice(tc * BLOCK, (tc + 1) * BLOCK)
            for kc in range(KC):
                last = product(to[:, :], (w_hi[n], w_lo[n]), (slice(None), slice(kc * P, (kc + 1) * P)),
                               (xn_hi, xn_lo), (slice(None), kc, cols), kc == 0, kc == KC - 1)
            return last

        @block.tensor
        def _(pe):
            def turn_lora_rows(b):
                pe.wait_ge(a_parts_done, b + 1)
                pe.wait_ge(a_hi_done, 2 * (b + 1))
                for c in range(BT):
                    last = nc.tensor.transpose(TV[0:PARTS, c * P:(c + 1) * P],
                                               a_parts[:, BT * b + c, :].bitcast(F32), ident[:, :])
                last.then_inc(a_turned, 1)

            def deltas(n, tiles):
                for c in tiles:
                    if c >= 2:
                        pe.wait_ge(h_ready, BT * n + c - 1)
                    nc.tensor.matmul((TK, TV)[c % 2][:, :],
                                     tile(aT, c), loraB[:, :],
                                     start=True, stop=True).then_inc(delta_done, 1)

            def turn_xn(n, banks, by_tile=False):
                b = n % BLOCKS
                if by_tile:
                    for c in range(BT):
                        pe.wait_ge(xn_ready, BT * n + c + 1)
                        for kc in range(KC):
                            turned = nc.tensor.transpose(tile(banks[kc], c), tile(acc[:, BT * b + c, :], kc),
                                                         ident[:, :])
                            if c == BT - 1:
                                turned.then_inc(xn_turned, 1)
                    return
                pe.wait_ge(xn_ready, BT * (n + 1))
                for kc in range(KC):
                    for c in range(BT):
                        last = nc.tensor.transpose(tile(banks[kc], c), tile(acc[:, BT * b + c, :], kc), ident[:, :])
                    last.then_inc(xn_turned, 1)

            def sum_squares(b, bank):
                pe.wait_ge(ssq_added, STEPS - BLOCKS + b + 1)
                for c in range(BT):
                    last = nc.tensor.matmul(bank[:, 2 * c:2 * c + 2], tile(ssq, BT * b + c), ones2[:, :],
                                            start=True, stop=True)
                last.then_inc(ss_summed, 1)

            pe.wait_ge(const_step, 3)
            turn_lora_rows(0)
            pe.wait_ge(aT_ready, 1)
            pe.wait_ge(b_ready, 1)
            deltas(0, range(BT))
            turn_xn(0, turn_banks, by_tile=True)

            def output(p, before=0):
                pe.wait_ge(masked, p.done)
                pe.wait_ge(states, p.states)
                pe.wait_ge(q_dec_done, p.done)
                if before:
                    pe.wait_ge(xn_lo_done, before)
                for c in range(BT):
                    inter = c >= first_state(p)
                    last = nc.tensor.matmul(tile(O, c), tile(v_tok, c), tile(scores, c), start=True, stop=not inter)
                    if inter:
                        last = nc.tensor.matmul(tile(O, c), state[:, c + BT * p.second, :], tile(q_dec, c),
                                                start=False, stop=True)
                last.then_inc(o_done, 1)

            def project_out(p):
                if p.tc == 0:
                    pe.wait_ge(w_ready["o"], p.head + 1)
                pe.wait_ge(o_lo_done, p.done)
                pe.wait_ge(sq_done, p.done)
                for c in range(BT):
                    product(y_bank[c][:, :], (o_hi, o_lo), (slice(None), slice(c * P, (c + 1) * P)),
                            (w_hi["o"], w_lo["o"]), (slice(None), slice(0, D)), True, True).then_inc(y_done, 1)

            def slot(i, kk, ln=None, rms=None, before=0):
                c = Step(i, kk)
                if ln is not None and ln < BLOCKS:
                    if not c.first_ever:
                        pe.wait_ge(v_tok_done, c.s)
                        pe.wait_ge(k_tok_done, c.s)
                    pe.wait_ge(xn_lo_done, KC * ln)
                    turn_lora_rows(ln)
                if rms is not None:
                    pe.wait_ge(v_tok_done, c.s)
                    if before:
                        pe.wait_ge(xn_lo_done, before - KC + 1)
                    sum_squares(rms, ss_bank(rms))
                if c.tc == 0:
                    pe.wait_ge(w_ready["k"], c.head + 1)
                pe.wait_ge(xn_lo_done, KC * (c.tc + 1))
                project(A, "k", c.tc).then_inc(proj["k"], 1)
                if ln is not None and ln < BLOCKS:
                    pe.wait_ge(aT_ready, ln + 1)
                    deltas(ln, (0, 1))
                if c.tc == 0:
                    pe.wait_ge(w_ready["v"], c.head + 1)
                if not c.first_ever:
                    pe.wait_ge(gate_done, c.s)
                project(B, "v", c.tc).then_inc(proj["v"], 1)
                if ln is not None and ln < BLOCKS:
                    deltas(ln, (2, 3))
                if not c.first_ever:
                    output(Step(i, kk - 1), before)
                pe.wait_ge(silu["k"], c.done)
                if not c.first_ever:
                    pe.wait_ge(k_tok_done, c.s)
                if ln is not None and ln < BLOCKS:
                    pe.wait_ge(h_ready, BT * (ln + 1))
                if rms is not None:
                    pe.wait_ge(o_var_ready, rms + 1)
                for n in range(BT):
                    last = nc.tensor.transpose(tile(TK, n), tile(k, n), ident[:, :])
                last.then_inc(k_turned, 1)
                pe.wait_ge(silu["v"], c.done)
                if not c.first_ever:
                    pe.wait_ge(v_tok_done, c.s)
                for n in range(BT):
                    last = nc.tensor.transpose(tile(TV, n), tile(v, n), ident[:, :])
                last.then_inc(v_turned, 1)
                if c.tc == 0:
                    pe.wait_ge(w_ready["q"], c.head + 1)
                project(A, "q", c.tc).then_inc(proj["q"], 1)
                if not c.first_ever:
                    project_out(Step(i, kk - 1))
                if c.tc == 0:
                    pe.wait_ge(w_ready["g"], c.head + 1)
                project(B, "g", c.tc).then_inc(proj["g"], 1)
                if ln is not None:
                    if not c.first_ever:
                        pe.wait_ge(y_added, BT * c.s)
                    pe.wait_ge(k_tok_done, c.done)
                    pe.wait_ge(v_tok_done, c.done)
                    turn_xn(ln, turn_banks)
                pe.wait_ge(silu["q"], c.done)
                if not c.first_ever:
                    pe.wait_ge(y_added, BT * (c.s - 1) + 1)
                for n in range(BT):
                    last = nc.tensor.matmul(tile(ST, n), tile(k, n), tile(q, n), start=True, stop=True)
                last.then_inc(scored, 1)
                pe.wait_ge(k_tok_done, c.done)
                pe.wait_ge(v_tok_done, c.done)
                if not c.first_ever:
                    pe.wait_ge(y_added, BT * c.s)
                for n in range(scans(c)):
                    last = nc.tensor.matmul(tile(KV, n), tile(k_tok, n), tile(v_tok, n), start=True, stop=True)
                last.then_inc(kv_done, 1)

            for kk in range(PEELED):
                slot(0, kk, ln=kk + 1, before=KC * (kk + 1))
            pe.wait_ge(xn_lo_done, KC * BLOCKS)
            with pe.Fori(0, HEADS - LAST_HEADS) as i:
                for kk in range(PEELED, PEELED + BLOCKS):
                    slot(i, kk)
            for kk in range(PEELED, LAST_HEADS * BLOCKS):
                early = kk - (LAST_HEADS * BLOCKS - 2)
                slot(HEADS - LAST_HEADS, kk, *((BLOCKS + early, early, KC * (BLOCKS + early)) if early >= 0 else ()))

            def f_project(c, which, n, done):
                if c.tc == 0:
                    pe.wait_ge(w_ready[n], HEADS + c.head + 1)
                if c.later:
                    pe.wait_ge(f_mul, c.s - 1)
                project(f_banks(c)[which], n, c.tc).then_inc(done, 1)

            def f_down_product(p, turned=None):
                if p.tc == 0:
                    pe.wait_ge(w_ready["o"], HEADS + p.head + 1)
                pe.wait_ge(f_lo, p.done)
                if not p.first_ever:
                    pe.wait_ge(d_added, BT * p.s)
                for c in range(BT):
                    if turned is not None and c >= 2:
                        pe.wait_ge(xn_lo_done, KC * turned + c - 1)
                    product(y_bank[c][:, :], (o_hi, o_lo), (slice(None), slice(c * P, (c + 1) * P)),
                            (w_hi["o"], w_lo["o"]), (slice(None), slice(0, D)), True, True).then_inc(d_done, 1)

            def f_slot(i, kk, ln=None, rms=None):
                c = Step(i, kk)
                pe.wait_ge(xn_lo_done, KC * (BLOCKS + c.tc + 1))
                f_project(c, 0, "k", fg_proj)
                if rms is not None:
                    pe.wait_ge(y_added, BT * STEPS)
                    sum_squares(rms, ss_bank(rms))
                    pe.wait_ge(o_var_ready, rms)
                f_project(c, 1, "v", fu_proj)
                if ln is not None:
                    pe.wait_ge(y_added, BT * STEPS)
                    pe.wait_ge(o_var_ready, BLOCKS)
                    pe.wait_ge(f_mul, c.s)
                    if c.later:
                        pe.wait_ge(d_added, BT * (c.s - 1))
                    turn_xn(ln, f_turn_banks(ln), by_tile=ln % BLOCKS == BLOCKS - 1)
                f_down_product(Step(i, kk - 1), ln)

            end, c = Step(HEADS - 1, BLOCKS - 1), Step(0, 0)
            pe.wait_ge(v_tok_done, STEPS)
            pe.wait_ge(xn_lo_done, KC * (BLOCKS + 2))
            sum_squares(2, ss_bank(2))
            f_project(c, 0, "k", fg_proj)
            output(end)
            pe.wait_ge(gate_done, STEPS)
            f_project(c, 1, "v", fu_proj)
            project_out(end)
            pe.wait_ge(k_tok_done, STEPS)
            f_slot(0, 1, ln=BLOCKS + 2, rms=3)
            f_slot(0, 2, ln=BLOCKS + 3)
            with pe.Fori(0, CHUNKS - 1) as i:
                for kk in range(PEELED, PEELED + BLOCKS):
                    f_slot(i, kk)
            f_slot(CHUNKS - 1, BLOCKS - 1)
            f_down_product(Step(CHUNKS - 1, BLOCKS - 1))


def kernel(x, L0_tok_W, L0_tok_lora_A, L0_tok_lora_B, L0_attn_slope_rate, L0_attn_w_qkv, L0_attn_w_gate,
           L0_attn_w_out, L0_attn_norm_w, L0_ffn_w_gate, L0_ffn_w_up, L0_ffn_w_down):
    import concourse.bacc as bacc
    from concourse.bass_utils import run_bass_kernel_spmd

    def by_input(w):
        w = np.asarray(w)
        n = w.shape[0] // P
        return w.reshape(n, P, KC, P).transpose(0, 3, 2, 1).reshape(n, P, KC * P)

    qkv = by_input(L0_attn_w_qkv)
    arrays = {
        "ids": np.asarray(x).reshape(TILES, P).T,
        "table": np.asarray(L0_tok_W),
        "lora_a": np.asarray(L0_tok_lora_A).T,
        "lora_b": np.asarray(L0_tok_lora_B).T,
        "slopes": np.asarray(L0_attn_slope_rate).reshape(1, HEADS),
        "norm_w": np.asarray(L0_attn_norm_w).reshape(HEADS, P).T,
        "w_qkv": qkv.reshape(HEADS, 3, P, D).transpose(1, 0, 2, 3),
        "w_gate": by_input(L0_attn_w_gate),
        "w_out": np.asarray(L0_attn_w_out).T.reshape(HEADS, P, D),
        "f_gate": by_input(L0_ffn_w_gate),
        "f_up": by_input(L0_ffn_w_up),
        "f_down": np.asarray(L0_ffn_w_down).T.reshape(CHUNKS, P, D),
    }
    arrays = {n: np.ascontiguousarray(a) for n, a in arrays.items()}
    nc = bacc.Bacc("TRN2", target_bir_lowering=False, num_devices=1)
    args = [nc.dram_tensor(n, a.shape, mybir.dt.from_np(a.dtype), kind="ExternalInput").ap()
            for n, a in arrays.items()]
    out = nc.dram_tensor("out", (T, D), F32, kind="ExternalOutput").ap()
    build(nc, *args, out)
    r = run_bass_kernel_spmd(nc, [arrays], core_ids=[0])
    return r.results[0]["out"].reshape(2, T // 2, D)
```

```python
from contextlib import ExitStack

import numpy as np
import concourse.bass as bass
from concourse import mybir
from concourse.alu_op_type import AluOpType as ALU

F32 = mybir.dt.float32
F32R = mybir.dt.float32r
I32 = mybir.dt.int32
ACT = mybir.ActivationFunctionType

P = 128
D = 512
KC = D // P
T = 2048
TILES = T // P
BLOCK = 512
BT = BLOCK // P
BLOCKS = T // BLOCK
SEQ_TILES = 1024 // P
HEADS = 16
INNER = HEADS * P
KINDS = "kqgo"
FFN_KINDS = "kgo"
GROUP = BLOCK // P
GROUPS = HEADS // GROUP
CHUNKS = 2048 // P
RANK = 16
PARTS = 96
SCALING = 32.0 / RANK
LN_EPS = 1e-5
RMS_EPS = 1e-6
STEPS = HEADS * BLOCKS
F_STEPS = CHUNKS * BLOCKS
PEELED = BLOCKS - 1
LAST_HEADS = 2
SCANS = SEQ_TILES - 1
SCALE_FIRST, SCALE_REST = (0, 1), (2, 3)
ROOT_OPS = 2 + 3 * 3
ROOT_MAGIC = 0x5F3759DF
LN_OPS = 2 * BT + ROOT_OPS + 2
RMS_OPS = ROOT_OPS
TAB = 2 * P + 1
DMA = 16


class Step:

    def __init__(self, i, k):
        self.s = BLOCKS * i + k
        self.done = self.s + 1
        self.tc = k % BLOCKS
        self.head = i + k // BLOCKS
        self.parity = k % 2
        self.of_parity = BLOCKS // 2 * i + k // 2 + 1
        self.second = self.tc % 2
        self.seq = 2 * self.head + self.tc // 2
        self.states = SCANS * self.seq + (SCANS if self.second else BT)
        static = isinstance(self.s, int)
        self.first_ever = static and self.s == 0
        self.later = not static or self.s > 1
        self.last_head = static and self.head == HEADS - 1


def build(nc, ids, table, lora_a, lora_b, slopes, norm_w, attn_w, ffn_w, v_store, out):
    with ExitStack() as ctx:
        def sb(name, shape, dt=F32):
            return ctx.enter_context(nc.sbuf_tensor(name, shape, dt))

        def sem(name):
            return ctx.enter_context(nc.semaphore(name))

        h = sb("h", [P, TILES, D])
        acc = sb("acc", [P, TILES, D])
        xn_hi = sb("xn_hi", [P, KC, T], F32R)
        xn_lo = sb("xn_lo", [P, KC, T], F32R)
        ssq = sb("ssq", [P, T])
        slope = sb("slope", [P, HEADS])
        normw = sb("normw", [P, HEADS])
        ident = sb("ident", [P, P])
        ones2 = sb("ones2", [P, 2])
        raw_all = sb("raw", [P, len(KINDS), D])
        w_hi_all, w_lo_all = sb("w_hi", [P, len(KINDS), D], F32R), sb("w_lo", [P, len(KINDS), D], F32R)
        raw, w_hi, w_lo = ({n: t[:, x, :] for x, n in enumerate(KINDS)} for t in (raw_all, w_hi_all, w_lo_all))
        exponent = sb("exponent", [P, TAB])
        tab = sb("tab", [P, TAB])
        decay_qk, decay_q, decay_k = tab[:, 0:P], tab[:, P:2 * P], tab[:, 2 * P:TAB]
        decay_chunk = tab[:, 2 * P - 1:2 * P]
        work = sb("work", [P, 8, BLOCK])
        k, q, q_dec, k_tok, scores, o, gate, sq = (work[:, x, :] for x in range(8))
        v_out = [work[:, 4 * x:4 * x + GROUP, :] for x in range(2)]
        v_toks = sb("v_toks", [P, 2, BLOCK])
        o_hi, o_lo = sb("o_hi", [P, BLOCK], F32R), sb("o_lo", [P, BLOCK], F32R)
        state = sb("state", [P, SEQ_TILES, P])
        idx = sb("idx", [P, TILES], I32)
        a_tok = sb("a_tok", [P, TILES, RANK])
        a_parts = sb("a_parts", [P, TILES, PARTS], F32R)
        stats = sb("stats", [P, BT, 6])
        mv = sb("mv", [P, BT, 2])
        var, newton, rstd, shift = (sb(n, [P, BT]) for n in ("var", "newton", "rstd", "shift"))
        o_var, o_newton, o_r = (sb(n, [P, BT]) for n in ("o_var", "o_newton", "o_r"))
        aT = sb("aT", [PARTS, BLOCK], F32R)
        loraB = sb("loraB", [PARTS, D], F32R)
        b_raw = scores[0:PARTS, :]
        exponent_i = acc[:, TILES - 2, 0:TAB].bitcast(I32)

        A, B, TK, TV, ST, KV, O, Y3 = (
            ctx.enter_context(nc.psum_tensor(f"bank_{n}", [P, BLOCK], F32))
            for n in ("a", "b", "tk", "tv", "st", "kv", "o", "y3"))
        y_bank = (ST, KV, O, Y3)

        idx_in, consts_in, const_step, exponents, tab_exp, tab_ready, acc_zero, ssq_zero = (
            sem(n) for n in ("idx_in", "consts_in", "const_step", "exponents",
                             "tab_exp", "tab_ready",
                             "acc_zero",
                             "ssq_zero"))
        a_gathered = [sem(f"a_gathered{b}") for b in range(BLOCKS)]
        gathered = [sem(f"gathered{t}") for t in range(TILES)]
        b_zeroed, b_in, b_hi_done, b_ready = (sem(n) for n in ("b_zeroed", "b_in", "b_hi_done", "b_ready"))
        a_zeroed = sem("a_zeroed")
        a_hi_done, a_parts_done = sem("a_hi_done"), sem("a_parts_done")
        a_turned, aT_ready = sem("a_turned"), sem("aT_ready")
        delta_done, h_ready, xn_ready = sem("delta_done"), sem("h_ready"), sem("xn_ready")
        acc_scaled, h_added = sem("acc_scaled"), sem("h_added")
        ln_op = sem("ln_op")
        xn_turned, xn_hi_done, xn_lo_done = (
            sem(n) for n in ("xn_turned", "xn_hi_done", "xn_lo_done"))
        ss_summed, o_var_ready = sem("ss_summed"), sem("o_var_ready")
        rms_op = sem("rms_op")

        loaded = {n: sem(f"loaded_{n}") for n in KINDS}
        w_hi_done = {n: sem(f"w_hi_done_{n}") for n in KINDS}
        w_ready = {n: sem(f"w_ready_{n}") for n in KINDS}
        v_projected, v_silu = sem("v_projected"), sem("v_silu")
        v_w_used = sem("v_w_used")
        v_stored = [sem(f"v_stored{x}") for x in range(2)]
        v_loaded = [sem(f"v_loaded{x}") for x in range(2)]

        proj = {n: sem(f"proj_{n}") for n in "kqg"}
        sigmoid = {n: sem(f"sigmoid_{n}") for n in "kq"}
        silu = {n: sem(f"silu_{n}") for n in "kq"}
        k_turned, k_tok_done, q_dec_done = sem("k_turned"), sem("k_tok_done"), sem("q_dec_done")
        scored, masked, kv_done, states = (
            sem(n) for n in ("scored", "masked", "kv_done",
                             "states"))
        o_done, gate_done, o_gated, sq_done, ssq_added, o_hi_done, o_lo_done = (
            sem(n) for n in ("o_done", "gate_done", "o_gated", "sq_done", "ssq_added", "o_hi_done", "o_lo_done"))
        y_done, y_added = sem("y_done"), sem("y_added")
        fg_proj, fu_proj, f_silu, f_mul, f_hi, f_lo = (
            sem(n) for n in ("fg_proj", "fu_proj", "f_silu", "f_mul", "f_hi", "f_lo"))
        d_done, d_added, out_done = sem("d_done"), sem("d_added"), sem("out_done")

        block = ctx.enter_context(nc.Block())

        def wait_apart(eng, semaphore, count, least=1):
            if not isinstance(count, int):
                eng.lower_val(count)
                eng.wait_ge(semaphore, least)
            eng.wait_ge(semaphore, count)

        def tile(ap, c):
            return ap[:, c * P:(c + 1) * P]

        def four(ap):
            return ap[:, :].rearrange("p (c n) -> p c n", c=BT)

        def tile3(ap, c):
            return ap[:, :, c * P:(c + 1) * P]

        def for_each_tile(ap):
            return ap.unsqueeze(1).broadcast_to([P, BT, P])

        def column(t, c):
            return t[:, bass.ds(c, 1)]

        def late_work(kk):
            early = kk - (LAST_HEADS * BLOCKS - 2)
            return (BLOCKS + early if early >= 0 else None), (early + 1 if early >= -1 else None)

        def first_state(c):
            return 0 if c.second else 1

        def scans(c):
            return SCANS - BT if c.second else BT

        def f_banks(c):
            return (TK, TV) if c.tc % 2 else (A, B)

        turn_banks = (TV, TK, O, Y3)
        late_banks = (O, TK, TV, Y3)
        v_banks = (A, B, ST, KV)

        def f_turn_banks(n):
            return (O, Y3) + ((TK, TV) if n % 2 else (A, B))

        @block.sync
        def _(sp):
            sp.dma_start(idx[:, :], ids).then_inc(idx_in, DMA)
            sp.wait_ge(b_zeroed, 1)
            for row in range(0, PARTS, 32):
                sp.dma_start(b_raw[row:row + RANK, :], lora_b).then_inc(b_in, DMA)
            for x, n in enumerate(KINDS):
                sp.dma_start(raw[n], attn_w[0, x]).then_inc(loaded[n], DMA)
            sp.dma_start(slope[:, :], slopes.broadcast_to([P, HEADS])).then_inc(consts_in, DMA)
            sp.dma_start(normw[:, :], norm_w).then_inc(consts_in, DMA)

            def load(n, src, count):
                wait_apart(sp, w_ready[n], count)
                sp.dma_start(raw[n], src.rearrange("a p n -> (a p) n")).then_inc(loaded[n], DMA)

            with sp.Fori(0, GROUPS) as g:
                for tc in range(BLOCKS):
                    wait_apart(sp, v_silu, TILES * g + BT * (tc + 1))
                    sp.dma_start(v_store[bass.ds(GROUP * g, GROUP), tc].rearrange("h p n -> p h n"), v_out[tc % 2]
                                 ).then_inc(v_stored[tc % 2], DMA)
                    if tc == 0:
                        for x, n in enumerate(KINDS):
                            load(n, attn_w[bass.ds(g + 1, 1), x], g + 1)
            with sp.Fori(1, HEADS) as i:
                for x, n in enumerate(KINDS):
                    load(n, attn_w[bass.ds(GROUPS + i, 1), x], GROUPS + i)
            with sp.Fori(0, CHUNKS) as j:
                for x, n in enumerate(FFN_KINDS):
                    load(n, ffn_w[bass.ds(j, 1), x], GROUPS + HEADS + j)
            for t in range(TILES):
                sp.wait_ge(d_added, BT * F_STEPS - TILES + t + 1)
                sp.dma_start(out[t * P:(t + 1) * P, :], h[:, t, :]).then_inc(out_done, DMA)
            sp.wait_ge(out_done, DMA * TILES)

        @block.gpsimd
        def _(pool):
            nc.gpsimd.memset(b_raw, 0.0).then_inc(b_zeroed, 1)
            nc.gpsimd.memset(a_parts[:, :, :].bitcast(F32), 0.0).then_inc(a_zeroed, 1)
            nc.gpsimd.iota(exponent_i[:, 0:P], pattern=[[-1, P]], base=0, channel_multiplier=1
                           ).then_inc(exponents, 1)
            nc.gpsimd.iota(exponent_i[:, P:2 * P], pattern=[[-1, P]], base=-1, channel_multiplier=0
                           ).then_inc(exponents, 1)
            nc.gpsimd.iota(exponent_i[:, 2 * P:TAB], pattern=[[1, 1]], base=1 - P, channel_multiplier=1
                           ).then_inc(exponents, 1)
            nc.gpsimd.memset(ident[:, :], 0.0).then_inc(const_step, 1)
            nc.gpsimd.memset(ones2[:, :], 1.0).then_inc(const_step, 1)

            def gather(b):
                tiles = range(BT * b, BT * (b + 1))
                row_of = {t: bass.IndirectOffsetOnAxis(idx[:, t:t + 1], 0) for t in tiles}
                for t in tiles:
                    nc.gpsimd.indirect_dma_start(a_tok[:, t, :], None, lora_a[:, :], row_of[t]
                                                 ).then_inc(a_gathered[b], DMA)
                for t in tiles:
                    nc.gpsimd.indirect_dma_start(h[:, t, :], None, table[:, :], row_of[t]
                                                 ).then_inc(gathered[t], DMA)

            def mask_table(c):
                wait_apart(pool, tab_exp, c.head + 1)
                nc.gpsimd.affine_select(out=decay_qk, in_=decay_qk, compare_op=ALU.is_ge, fill=0.0, base=0,
                                        pattern=[[1, P]], channel_multiplier=-1).then_inc(tab_ready, 1)

            pool.wait_ge(const_step, 2)
            nc.gpsimd.affine_select(out=ident[:, :], in_=ident[:, :], compare_op=ALU.not_equal, fill=1.0, base=0,
                                    pattern=[[-1, P]], channel_multiplier=1).then_inc(const_step, 1)
            pool.wait_ge(idx_in, DMA)
            gather(0)
            pool.wait_ge(exponents, 3)
            nc.gpsimd.tensor_scalar(exponent[:, :], exponent_i, 0.0, None, ALU.min).then_inc(exponents, 1)
            mask_table(Step(0, 0))
            for b in range(1, BLOCKS):
                gather(b)
            nc.gpsimd.memset(ssq[:, :], 0.0).then_inc(ssq_zero, 1)

            def zero_acc(b):
                pool.wait_ge(xn_turned, KC * (b + 1))
                nc.gpsimd.memset(acc[:, BT * b:BT * (b + 1), :], 0.0).then_inc(acc_zero, 1)

            def add_squares(p):
                cols = ssq[:, p.tc * BLOCK:(p.tc + 1) * BLOCK]
                pool.wait_ge(sq_done, p.done)
                nc.gpsimd.tensor_tensor(cols, cols, sq[:, :], ALU.add).then_inc(ssq_added, 1)

            def add_scaled(b):
                for c in SCALE_REST:
                    t = BT * b + c
                    pool.wait_ge(acc_scaled, len(SCALE_REST) * b + c - SCALE_REST[0] + 1)
                    nc.gpsimd.tensor_tensor(h[:, t, :], acc[:, t, :], h[:, t, :], ALU.add).then_inc(h_added, 1)

            def split_low(n, count):
                pool.wait_ge(w_hi_done[n], count)
                nc.gpsimd.tensor_tensor(w_lo[n][:, :], raw[n][:, :], w_hi[n][:, :].bitcast(F32),
                                        ALU.subtract).then_inc(w_ready[n], 1)

            def slot(i, kk, rms=None):
                c = Step(i, kk)
                if c.tc == 0 and not c.first_ever:
                    mask_table(c)
                if not c.first_ever:
                    add_squares(Step(i, kk - 1))
                if c.tc == BLOCKS - 1:
                    split_low("k", GROUPS + c.head + 2)
                pool.wait_ge(silu["q"], c.done)
                nc.gpsimd.tensor_tensor(four(q_dec), four(q), for_each_tile(decay_q), ALU.mult
                                        ).then_inc(q_dec_done, 1)
                if c.tc == BLOCKS - 1:
                    for n in "g" if c.last_head else "qg":
                        split_low(n, GROUPS + c.head + 2)
                if rms is not None:
                    add_scaled(rms)
                if c.tc == 0 and not c.first_ever:
                    split_low("o", GROUPS + c.head + 1)

            for b in range(BLOCKS):
                zero_acc(b)
            pool.wait_ge(ssq_zero, 1)
            for kk in range(PEELED):
                slot(0, kk)
            with pool.Fori(0, HEADS - LAST_HEADS) as i:
                for kk in range(PEELED, PEELED + BLOCKS):
                    slot(i, kk)
            for kk in range(PEELED, LAST_HEADS * BLOCKS):
                slot(HEADS - LAST_HEADS, kk, late_work(kk)[1])
            add_squares(Step(HEADS - 1, BLOCKS - 1))
            split_low("o", GROUPS + HEADS + 1)
            add_scaled(BLOCKS - 1)
            with pool.Fori(1, CHUNKS) as j:
                for n in FFN_KINDS:
                    split_low(n, GROUPS + HEADS + j + 1)

        @block.scalar
        def _(act):
            def decay_table(c):
                act_waits = (("states", states, SCANS * c.seq), ("masked", masked, c.s), ("q_dec", q_dec_done, c.s))
                if not c.first_ever:
                    for _, used, count in act_waits:
                        wait_apart(act, used, count)
                nc.scalar.activation(tab[:, :], exponent[:, :], ACT.Exp, scale=column(slope, c.head)
                                     ).then_inc(tab_exp, 1)

            def split_high(n, count):
                act.wait_ge(loaded[n], DMA * count)
                nc.scalar.copy(w_hi[n][:, :], raw[n][:, :]).then_inc(w_hi_done[n], 1)

            def normalise(n):
                act.wait_ge(ln_op, LN_OPS * (n + 1))
                for c in range(BT):
                    t = BT * (n % BLOCKS) + c
                    nc.scalar.activation(acc[:, t, :], h[:, t, :], ACT.Identity, scale=rstd[:, c:c + 1],
                                         bias=shift[:, c:c + 1]).then_inc(xn_ready, 1)

            def scale_rest(b):
                act.wait_ge(rms_op, RMS_OPS * (b + 1))
                for c in SCALE_REST:
                    nc.scalar.activation(acc[:, BT * b + c, :], acc[:, BT * b + c, :], ACT.Copy, scale=o_r[:, c:c + 1]
                                         ).then_inc(acc_scaled, 1)

            def xn_high(n, banks):
                b = n % BLOCKS
                for kc in range(KC):
                    act.wait_ge(xn_turned, KC * n + kc + 1)
                    nc.scalar.copy(xn_hi[:, kc, b * BLOCK:(b + 1) * BLOCK], banks[kc][:, :]).then_inc(xn_hi_done, 1)

            def squares(p):
                if not p.first_ever:
                    act.wait_ge(ssq_added, p.s)
                nc.scalar.activation(sq[:, :], O[:, :], ACT.Square).then_inc(sq_done, 1)

            def o_high(p):
                act.wait_ge(o_gated, p.done)
                if not p.first_ever:
                    act.wait_ge(y_done, BT * p.s)
                nc.scalar.copy(o_hi[:, :], o[:, :]).then_inc(o_hi_done, 1)

            def keep_lora_rows(b):
                act.wait_ge(a_turned, b + 1)
                if b:
                    act.wait_ge(delta_done, BT * b)
                nc.scalar.copy(aT[:, :], TV[0:PARTS, :]).then_inc(aT_ready, 1)

            def lora_high(b):
                act.wait_ge(a_gathered[b], BT * DMA)
                act.wait_ge(a_zeroed, 1)
                for col in (0, 32):
                    nc.scalar.copy(a_parts[:, BT * b:BT * (b + 1), col:col + RANK], a_tok[:, BT * b:BT * (b + 1), :]
                                   ).then_inc(a_hi_done, 1)

            act.wait_ge(b_in, 3 * DMA)
            nc.scalar.copy(loraB[:, :], b_raw).then_inc(b_hi_done, 1)
            for n in "kq":
                split_high(n, 1)
            lora_high(0)
            keep_lora_rows(0)
            act.wait_ge(exponents, 4)
            act.wait_ge(consts_in, 2 * DMA)
            decay_table(Step(0, 0))
            for n in "go":
                split_high(n, 1)
            lora_high(1)
            keep_lora_rows(1)
            normalise(0)
            xn_high(0, turn_banks)

            def v_tiles(g, tc, tiles):
                for c in tiles:
                    if c == 0 and (tc >= 2 or not isinstance(g, int)):
                        act.wait_ge(v_stored[tc % 2], DMA * (2 * g + tc // 2))
                    act.wait_ge(v_projected, TILES * g + BT * tc + c + 1)
                    nc.scalar.activation(tile3(v_out[tc % 2], c), four(v_banks[c]), ACT.Silu).then_inc(v_silu, 1)

            def v_block(g, tc):
                first = isinstance(g, int)
                norm, delta = tc + 1, tc + 2
                if first and delta < BLOCKS:
                    lora_high(delta)
                v_tiles(g, tc, (0,))
                if first and delta < BLOCKS:
                    keep_lora_rows(delta)
                v_tiles(g, tc, (1,))
                if first and norm < BLOCKS:
                    normalise(norm)
                v_tiles(g, tc, (2,))
                if first and norm < BLOCKS:
                    xn_high(norm, turn_banks)
                if tc == BLOCKS - 1:
                    for x, n in enumerate(KINDS[:-1]):
                        act.wait_ge(v_w_used, (KC - 1) * g + x + 1)
                        split_high(n, g + 2)
                v_tiles(g, tc, (3,))
                if tc == BLOCKS - 1:
                    split_high(KINDS[-1], g + 2)

            for tc in range(BLOCKS):
                v_block(0, tc)
            with act.Fori(1, GROUPS) as g:
                for tc in range(BLOCKS):
                    v_block(g, tc)

            def load_v(c):
                act.dma_start(v_toks[:, c.parity, :], v_store[bass.ds(c.head, 1), c.tc].rearrange("a p n -> (a p) n")
                              ).then_inc(v_loaded[c.parity], DMA)

            act.wait_ge(v_stored[0], DMA * GROUPS * BLOCKS // 2)
            act.wait_ge(v_stored[1], DMA)
            load_v(Step(0, 0))
            load_v(Step(0, 1))

            def slot(i, kk, ln=None, rms=None):
                c = Step(i, kk)
                last_ever = c.last_head and c.tc == BLOCKS - 1
                act.wait_ge(proj["k"], c.done)
                if not c.first_ever:
                    act.wait_ge(scored, c.s)
                nc.scalar.activation(k[:, :], A[:, :], ACT.Sigmoid).then_inc(sigmoid["k"], 1)
                if c.tc == 0 and not c.first_ever:
                    decay_table(c)
                if not c.first_ever:
                    o_high(Step(i, kk - 1))
                    squares(Step(i, kk - 1))
                    if not last_ever:
                        load_v(Step(i, kk + 1))
                act.wait_ge(k_turned, c.done)
                if not c.first_ever:
                    act.wait_ge(kv_done, c.s)
                if c.tc == 0:
                    act.wait_ge(tab_exp, c.head + 1)
                nc.scalar.activation(k_tok[:, :], TK[:, :], ACT.Copy, scale=decay_k).then_inc(k_tok_done, 1)
                act.wait_ge(proj["q"], c.done)
                if not c.first_ever:
                    act.wait_ge(q_dec_done, c.s)
                nc.scalar.activation(q[:, :], A[:, :], ACT.Sigmoid).then_inc(sigmoid["q"], 1)
                if c.tc == BLOCKS - 1:
                    for n in "k" if c.last_head else "kq":
                        split_high(n, GROUPS + c.head + 2)
                if ln is not None:
                    normalise(ln)
                    xn_high(ln, late_banks)
                if rms is not None:
                    scale_rest(rms)
                if c.first_ever:
                    act.wait_ge(v_stored[1], DMA * GROUPS * BLOCKS // 2)
                act.wait_ge(proj["g"], c.done)
                nc.scalar.activation(gate[:, :], B[:, :], ACT.Sigmoid).then_inc(gate_done, 1)
                if c.tc == BLOCKS - 1:
                    split_high("g", GROUPS + c.head + 2)
                if c.tc == 0 and not c.first_ever:
                    act.wait_ge(y_done, BT * c.s)
                    split_high("o", GROUPS + c.head + 1)

            for kk in range(PEELED):
                slot(0, kk)
            with act.Fori(0, HEADS - LAST_HEADS) as i:
                for kk in range(PEELED, PEELED + BLOCKS):
                    slot(i, kk)
            for kk in range(PEELED, LAST_HEADS * BLOCKS):
                slot(HEADS - LAST_HEADS, kk, *late_work(kk))
            end = Step(HEADS - 1, BLOCKS - 1)
            o_high(end)
            squares(end)

            def f_silu_of(c):
                act.wait_ge(fg_proj, c.done)
                if not c.first_ever:
                    act.wait_ge(f_mul, c.s)
                nc.scalar.activation(gate[:, :], f_banks(c)[0][:, :], ACT.Silu).then_inc(f_silu, 1)

            def f_high(c):
                act.wait_ge(f_mul, c.done)
                if c.first_ever:
                    act.wait_ge(y_done, BT * STEPS)
                else:
                    act.wait_ge(d_done, BT * c.s)
                nc.scalar.copy(o_hi[:, :], o[:, :]).then_inc(f_hi, 1)

            def f_slot(i, kk, norm=None, turned=None):
                c = Step(i, kk)
                f_silu_of(c)
                if c.first_ever:
                    act.wait_ge(y_done, BT * STEPS)
                    split_high("o", GROUPS + HEADS + 1)
                if norm is not None:
                    normalise(norm)
                if turned is not None:
                    xn_high(turned, f_turn_banks(turned))
                if turned == BLOCKS + 2:
                    scale_rest(3)
                if c.tc == BLOCKS - 1 and not c.last_head:
                    split_high("k", GROUPS + HEADS + c.head + 2)
                f_high(c)
                if c.tc == 0 and not c.first_ever:
                    split_high("o", GROUPS + HEADS + c.head + 1)
                if c.tc == BLOCKS - 1 and not c.last_head:
                    act.wait_ge(fu_proj, c.done)
                    split_high("g", GROUPS + HEADS + c.head + 2)

            f_slot(0, 0, norm=BLOCKS + 2)
            f_slot(0, 1, turned=BLOCKS + 2)
            f_slot(0, 2, norm=BLOCKS + 3, turned=BLOCKS + 3)
            with act.Fori(0, CHUNKS - 1) as i:
                for kk in range(PEELED, PEELED + BLOCKS):
                    f_slot(i, kk)
            f_slot(CHUNKS - 1, BLOCKS - 1)

        @block.vector
        def _(dve):
            def add_deltas(n, banks, tiles=range(BT)):
                for c in tiles:
                    t = BT * n + c
                    dve.wait_ge(delta_done, t + 1)
                    dve.wait_ge(gathered[t], DMA)
                    nc.vector.scalar_tensor_tensor(h[:, t, :], banks[c][:, :], SCALING, h[:, t, :],
                                                   ALU.mult, ALU.add).then_inc(h_ready, 1)

            def inverse_root(y, tmp, x, op, ops):
                bits = tmp[:, :].bitcast(I32)
                nc.vector.tensor_scalar(bits, x[:, :].bitcast(I32), 1, None, ALU.logical_shift_right).then_inc(op, 1)
                dve.wait_ge(op, ops + 1)
                nc.vector.tensor_scalar(y[:, :].bitcast(I32), bits, -1.0, float(ROOT_MAGIC), ALU.mult, ALU.add
                                        ).then_inc(op, 1)
                for n in range(ops + 2, ops + ROOT_OPS, 3):
                    dve.wait_ge(op, n)
                    nc.vector.tensor_tensor(tmp[:, :], y[:, :], y[:, :], ALU.mult).then_inc(op, 1)
                    dve.wait_ge(op, n + 1)
                    nc.vector.scalar_tensor_tensor(tmp[:, :], tmp[:, :], -0.5, x[:, :], ALU.mult, ALU.mult
                                                   ).then_inc(op, 1)
                    dve.wait_ge(op, n + 2)
                    nc.vector.scalar_tensor_tensor(y[:, :], tmp[:, :], 1.5, y[:, :], ALU.add, ALU.mult
                                                   ).then_inc(op, 1)

            def mean_square(b):
                sums = TV[:, 0:2 * BT].rearrange("p (t a) -> p t a", a=2)[:, :, 0]
                dve.wait_ge(ss_summed, b + 1)
                nc.vector.tensor_scalar(o_var[:, :], sums, 1.0 / INNER, RMS_EPS, ALU.mult, ALU.add
                                        ).then_inc(o_var_ready, 1)

            def rms_factor(b):
                dve.wait_ge(o_var_ready, b + 1)
                if b:
                    dve.wait_ge(acc_scaled, len(SCALE_REST) * b)
                inverse_root(o_r, o_newton, o_var, rms_op, RMS_OPS * b)

            def scale_and_add(b):
                dve.wait_ge(rms_op, RMS_OPS * (b + 1))
                for c in SCALE_FIRST:
                    t = BT * b + c
                    nc.vector.scalar_tensor_tensor(h[:, t, :], acc[:, t, :], o_r[:, c:c + 1], h[:, t, :],
                                                   ALU.mult, ALU.add).then_inc(h_ready, 1)

            def statistics(n, tiles):
                for c in tiles:
                    if n < BLOCKS:
                        dve.wait_ge(h_ready, BT * n + c + 1)
                    elif c in SCALE_FIRST:
                        dve.wait_ge(h_ready, TILES + len(SCALE_FIRST) * (n - BLOCKS) + c + 1)
                    else:
                        dve.wait_ge(h_added, len(SCALE_REST) * (n - BLOCKS) + c - SCALE_REST[0] + 1)
                    if n and not c:
                        dve.wait_ge(ln_op, LN_OPS * n)
                    nc.vector.bn_stats(stats[:, c, :], h[:, BT * (n % BLOCKS) + c, :]).then_inc(ln_op, 1)

            def scale_and_shift(n):
                ops = LN_OPS * n
                if n:
                    dve.wait_ge(xn_ready, BT * n)
                for c in range(BT):
                    dve.wait_ge(ln_op, ops + c + 1)
                    nc.vector.bn_aggr(mv[:, c, :], stats[:, c, :]).then_inc(ln_op, 1)
                ops += 2 * BT
                dve.wait_ge(ln_op, ops)
                nc.vector.tensor_scalar(var[:, :], mv[:, :, 1], LN_EPS, None, ALU.add).then_inc(ln_op, 1)
                dve.wait_ge(ln_op, ops + 1)
                inverse_root(rstd, newton, var, ln_op, ops + 1)
                dve.wait_ge(ln_op, ops + 1 + ROOT_OPS)
                nc.vector.scalar_tensor_tensor(shift[:, :], mv[:, :, 0], -1.0, rstd[:, :], ALU.mult, ALU.mult
                                               ).then_inc(ln_op, 1)

            def xn_low(n, banks):
                cols = slice((n % BLOCKS) * BLOCK, (n % BLOCKS + 1) * BLOCK)
                for kc in range(KC):
                    dve.wait_ge(xn_hi_done, KC * n + kc + 1)
                    nc.vector.tensor_tensor(xn_lo[:, kc, cols], banks[kc][:, :], xn_hi[:, kc, cols].bitcast(F32),
                                            ALU.subtract).then_inc(xn_lo_done, 1)

            def silu_of(n, c):
                dve.wait_ge(sigmoid[n], c.done)
                x = {"k": k, "q": q}[n]
                nc.vector.tensor_tensor(x[:, :], A[:, :], x[:, :], ALU.mult).then_inc(silu[n], 1)

            def gate_output(p):
                dve.wait_ge(o_done, p.done)
                dve.wait_ge(gate_done, p.done)
                if not p.first_ever:
                    dve.wait_ge(o_hi_done, p.s)
                    dve.wait_ge(o_lo_done, p.s)
                nc.vector.scalar_tensor_tensor(o[:, :], O[:, :], column(normw, p.head), gate[:, :],
                                               ALU.mult, ALU.mult).then_inc(o_gated, 1)

            def o_low(p):
                dve.wait_ge(o_hi_done, p.done)
                nc.vector.tensor_tensor(o_lo[:, :], o[:, :], o_hi[:, :].bitcast(F32), ALU.subtract
                                        ).then_inc(o_lo_done, 1)

            def add_projection(p):
                for c in range(BT):
                    t = BT * p.tc + c
                    dve.wait_ge(y_done, BT * p.s + c + 1)
                    nc.vector.tensor_tensor(acc[:, t, :], y_bank[c][:, :], acc[:, t, :], ALU.add
                                            ).then_inc(y_added, 1)

            def slot(i, kk, ln=None, rms=None):
                c = Step(i, kk)
                silu_of("k", c)
                if not c.first_ever:
                    gate_output(Step(i, kk - 1))
                    if ln is not None:
                        scale_and_add(ln - BLOCKS)
                    o_low(Step(i, kk - 1))
                if ln is not None:
                    statistics(ln, (0, 1))
                silu_of("q", c)
                if ln is not None:
                    statistics(ln, (2, 3))
                    scale_and_shift(ln)
                if not c.first_ever:
                    if isinstance(c.s, int) and c.s <= PEELED:
                        dve.wait_ge(acc_zero, c.s)
                    add_projection(Step(i, kk - 1))
                if rms is not None:
                    mean_square(rms)
                    rms_factor(rms)
                if c.tc == 0:
                    dve.wait_ge(tab_ready, c.head + 1)
                if c.first_ever:
                    dve.wait_ge(v_stored[1], DMA * GROUPS * BLOCKS // 2)
                dve.wait_ge(scored, c.done)
                nc.vector.tensor_tensor(four(scores), four(ST), for_each_tile(decay_qk), ALU.mult
                                        ).then_inc(masked, 1)
                dve.wait_ge(kv_done, c.done)
                for n in range(scans(c)):
                    at = n + BT * c.second
                    if at == 0:
                        nc.vector.tensor_copy(state[:, 1, :], tile(KV, 0)).then_inc(states, 1)
                    else:
                        dve.wait_ge(states, SCANS * c.seq + at)
                        nc.vector.scalar_tensor_tensor(state[:, at + 1, :], state[:, at, :], decay_chunk,
                                                       tile(KV, n), ALU.mult, ALU.add).then_inc(states, 1)
                if ln is not None:
                    xn_low(ln, late_banks)

            def split_low(n, count):
                dve.wait_ge(w_hi_done[n], count)
                nc.vector.tensor_tensor(w_lo[n][:, :], raw[n][:, :], w_hi[n][:, :].bitcast(F32), ALU.subtract
                                        ).then_inc(w_ready[n], 1)

            def lora_low(b):
                tiles = slice(BT * b, BT * (b + 1))
                dve.wait_ge(a_hi_done, 2 * b + 1)
                nc.vector.tensor_tensor(a_parts[:, tiles, 64:64 + RANK], a_tok[:, tiles, :],
                                        a_parts[:, tiles, 0:RANK].bitcast(F32), ALU.subtract
                                        ).then_inc(a_parts_done, 1)

            dve.wait_ge(b_hi_done, 1)
            nc.vector.tensor_tensor(loraB[32:64, :], b_raw[32:64, :], loraB[32:64, :].bitcast(F32), ALU.subtract
                                    ).then_inc(b_ready, 1)
            for n in "kq":
                split_low(n, 1)
            lora_low(0)
            for c in range(BT):
                add_deltas(0, turn_banks, (c,))
                statistics(0, (c,))
            lora_low(1)
            scale_and_shift(0)
            for n in "go":
                split_low(n, 1)
            add_deltas(1, v_banks)
            xn_low(0, turn_banks)
            for ln in range(1, BLOCKS):
                if ln + 1 < BLOCKS:
                    lora_low(ln + 1)
                statistics(ln, range(BT))
                scale_and_shift(ln)
                if ln + 1 < BLOCKS:
                    add_deltas(ln + 1, turn_banks)
                xn_low(ln, turn_banks)
            with dve.Fori(0, GROUPS) as g:
                for n in KINDS:
                    split_low(n, g + 2)
            for kk in range(PEELED):
                slot(0, kk)
            dve.wait_ge(acc_zero, BLOCKS)
            with dve.Fori(0, HEADS - LAST_HEADS) as i:
                for kk in range(PEELED, PEELED + BLOCKS):
                    slot(i, kk)
            for kk in range(PEELED, LAST_HEADS * BLOCKS):
                slot(HEADS - LAST_HEADS, kk, *late_work(kk))
            end = Step(HEADS - 1, BLOCKS - 1)
            def f_multiply(c):
                dve.wait_ge(fu_proj, c.done)
                dve.wait_ge(f_silu, c.done)
                if c.first_ever:
                    dve.wait_ge(o_hi_done, STEPS)
                    dve.wait_ge(o_lo_done, STEPS)
                else:
                    dve.wait_ge(f_hi, c.s)
                    dve.wait_ge(f_lo, c.s)
                nc.vector.tensor_tensor(o[:, :], f_banks(c)[1][:, :], gate[:, :], ALU.mult).then_inc(f_mul, 1)

            def f_low(c):
                dve.wait_ge(f_hi, c.done)
                nc.vector.tensor_tensor(o_lo[:, :], o[:, :], o_hi[:, :].bitcast(F32), ALU.subtract
                                        ).then_inc(f_lo, 1)

            def add_down(p):
                for c in range(BT):
                    t = BT * p.tc + c
                    dve.wait_ge(d_done, BT * p.s + c + 1)
                    nc.vector.tensor_tensor(h[:, t, :], y_bank[c][:, :], h[:, t, :], ALU.add).then_inc(d_added, 1)

            def f_slot(i, kk):
                f_multiply(Step(i, kk))
                add_down(Step(i, kk - 1))
                f_low(Step(i, kk))

            first, second, third = (Step(0, kk) for kk in range(PEELED))
            gate_output(end)
            scale_and_add(2)
            o_low(end)
            statistics(BLOCKS + 2, range(BT))
            f_multiply(first)
            scale_and_shift(BLOCKS + 2)
            mean_square(3)
            add_projection(end)
            f_low(first)
            rms_factor(3)
            xn_low(BLOCKS + 2, f_turn_banks(BLOCKS + 2))
            scale_and_add(3)
            f_multiply(second)
            statistics(BLOCKS + 3, range(BT))
            scale_and_shift(BLOCKS + 3)
            add_down(first)
            f_low(second)
            f_multiply(third)
            xn_low(BLOCKS + 3, f_turn_banks(BLOCKS + 3))
            add_down(second)
            f_low(third)
            with dve.Fori(0, CHUNKS - 1) as i:
                for kk in range(PEELED, PEELED + BLOCKS):
                    f_slot(i, kk)
            f_slot(CHUNKS - 1, BLOCKS - 1)
            add_down(Step(CHUNKS - 1, BLOCKS - 1))

        def product(to, w, w_at, x, x_at, start, stop):
            nc.tensor.matmul(to, w[0][w_at], x[0][x_at], start=start, stop=False)
            nc.tensor.matmul(to, w[0][w_at], x[1][x_at], start=False, stop=False)
            return nc.tensor.matmul(to, w[1][w_at], x[0][x_at], start=False, stop=stop)

        def project(to, n, tc):
            cols = slice(tc * BLOCK, (tc + 1) * BLOCK)
            for kc in range(KC):
                last = product(to[:, :], (w_hi[n], w_lo[n]), (slice(None), slice(kc * P, (kc + 1) * P)),
                               (xn_hi, xn_lo), (slice(None), kc, cols), kc == 0, kc == KC - 1)
            return last

        @block.tensor
        def _(pe):
            def turn_lora_rows(b):
                pe.wait_ge(a_parts_done, b + 1)
                pe.wait_ge(a_hi_done, 2 * (b + 1))
                for c in range(BT):
                    last = nc.tensor.transpose(TV[0:PARTS, c * P:(c + 1) * P],
                                               a_parts[:, BT * b + c, :].bitcast(F32), ident[:, :])
                last.then_inc(a_turned, 1)

            def deltas(n, banks):
                for c in range(BT):
                    nc.tensor.matmul(banks[c][:, :],
                                     tile(aT, c), loraB[:, :],
                                     start=True, stop=True).then_inc(delta_done, 1)

            def turn_xn(n, banks, by_tile=False):
                b = n % BLOCKS
                if by_tile:
                    for c in range(BT):
                        pe.wait_ge(xn_ready, BT * n + c + 1)
                        for kc in range(KC):
                            turned = nc.tensor.transpose(tile(banks[kc], c), tile(acc[:, BT * b + c, :], kc),
                                                         ident[:, :])
                            if c == BT - 1:
                                turned.then_inc(xn_turned, 1)
                    return
                pe.wait_ge(xn_ready, BT * (n + 1))
                for kc in range(KC):
                    for c in range(BT):
                        last = nc.tensor.transpose(tile(banks[kc], c), tile(acc[:, BT * b + c, :], kc), ident[:, :])
                    last.then_inc(xn_turned, 1)

            def sum_squares(b):
                pe.wait_ge(ssq_added, STEPS - BLOCKS + b + 1)
                for c in range(BT):
                    last = nc.tensor.matmul(TV[:, 2 * c:2 * c + 2], tile(ssq, BT * b + c), ones2[:, :],
                                            start=True, stop=True)
                last.then_inc(ss_summed, 1)

            pe.wait_ge(const_step, 3)
            turn_lora_rows(0)
            pe.wait_ge(aT_ready, 1)
            pe.wait_ge(b_ready, 1)
            deltas(0, turn_banks)
            pe.wait_ge(h_ready, BT)
            turn_lora_rows(1)
            pe.wait_ge(aT_ready, 2)
            deltas(1, v_banks)
            turn_xn(0, turn_banks, by_tile=True)

            def v_tile(g, tc, c):
                if tc or not isinstance(g, int):
                    pe.wait_ge(v_silu, TILES * g + BT * (tc - 1) + c + 1)
                for kc in range(KC):
                    if tc == 0 and c == 0:
                        pe.wait_ge(w_ready[KINDS[kc]], g + 1)
                    last = product(v_banks[c][:, :], (xn_hi, xn_lo),
                                   (slice(None), kc, slice((BT * tc + c) * P, (BT * tc + c + 1) * P)),
                                   (w_hi_all, w_lo_all), (slice(None), kc, slice(None)), kc == 0, kc == KC - 1)
                    if tc == BLOCKS - 1 and c == BT - 1 and kc < KC - 1:
                        last.then_inc(v_w_used, 1)
                last.then_inc(v_projected, 1)

            def v_block(g, tc):
                first = isinstance(g, int)
                norm, delta = tc + 1, tc + 2
                if first:
                    pe.wait_ge(xn_lo_done, KC * (tc + 1))
                    if tc == 0:
                        pe.wait_ge(h_ready, 2 * BT)
                v_tile(g, tc, 0)
                if first and delta < BLOCKS:
                    turn_lora_rows(delta)
                v_tile(g, tc, 1)
                if first and delta < BLOCKS:
                    pe.wait_ge(aT_ready, delta + 1)
                    deltas(delta, turn_banks)
                v_tile(g, tc, 2)
                if first and norm < BLOCKS:
                    pe.wait_ge(h_ready, BT * min(delta + 1, BLOCKS))
                    turn_xn(norm, turn_banks)
                v_tile(g, tc, 3)

            for tc in range(BLOCKS):
                v_block(0, tc)
            with pe.Fori(1, GROUPS) as g:
                for tc in range(BLOCKS):
                    v_block(g, tc)

            def output(p, before=0):
                pe.wait_ge(masked, p.done)
                pe.wait_ge(states, p.states)
                pe.wait_ge(q_dec_done, p.done)
                if before:
                    pe.wait_ge(xn_lo_done, before - KC + 1)
                for c in range(BT):
                    inter = c >= first_state(p)
                    last = nc.tensor.matmul(tile(O, c), tile(v_toks[:, p.parity, :], c), tile(scores, c),
                                            start=True, stop=not inter)
                    if inter:
                        last = nc.tensor.matmul(tile(O, c), state[:, c + BT * p.second, :], tile(q_dec, c),
                                                start=False, stop=True)
                last.then_inc(o_done, 1)

            def project_out(p):
                if p.tc == 0:
                    pe.wait_ge(w_ready["o"], GROUPS + p.head + 1)
                pe.wait_ge(o_lo_done, p.done)
                for c in range(BT):
                    if y_bank[c] is O:
                        pe.wait_ge(sq_done, p.done)
                    product(y_bank[c][:, :], (o_hi, o_lo), (slice(None), slice(c * P, (c + 1) * P)),
                            (w_hi["o"], w_lo["o"]), (slice(None), slice(0, D)), True, True).then_inc(y_done, 1)

            def slot(i, kk, ln=None, rms=None, before=0):
                c = Step(i, kk)
                if c.tc == 0:
                    pe.wait_ge(w_ready["k"], GROUPS + c.head + 1)
                if c.first_ever:
                    pe.wait_ge(v_silu, TILES * GROUPS)
                project(A, "k", c.tc).then_inc(proj["k"], 1)
                if not c.first_ever:
                    output(Step(i, kk - 1), before)
                pe.wait_ge(silu["k"], c.done)
                if not c.first_ever:
                    pe.wait_ge(k_tok_done, c.s)
                if before:
                    pe.wait_ge(xn_lo_done, before)
                for n in range(BT):
                    last = nc.tensor.transpose(tile(TK, n), tile(k, n), ident[:, :])
                last.then_inc(k_turned, 1)
                if c.tc == 0:
                    pe.wait_ge(w_ready["q"], GROUPS + c.head + 1)
                project(A, "q", c.tc).then_inc(proj["q"], 1)
                if not c.first_ever:
                    project_out(Step(i, kk - 1))
                if rms is not None:
                    if rms:
                        pe.wait_ge(o_var_ready, rms)
                    sum_squares(rms)
                if c.tc == 0:
                    pe.wait_ge(w_ready["g"], GROUPS + c.head + 1)
                if not c.first_ever:
                    pe.wait_ge(gate_done, c.s)
                project(B, "g", c.tc).then_inc(proj["g"], 1)
                pe.wait_ge(silu["q"], c.done)
                if not c.first_ever:
                    pe.wait_ge(y_added, BT * (c.s - 1) + 1)
                for n in range(BT):
                    last = nc.tensor.matmul(tile(ST, n), tile(k, n), tile(q, n), start=True, stop=True)
                last.then_inc(scored, 1)
                pe.wait_ge(k_tok_done, c.done)
                pe.wait_ge(v_loaded[c.parity], DMA * c.of_parity)
                if not c.first_ever:
                    pe.wait_ge(y_added, BT * c.s)
                for n in range(scans(c)):
                    last = nc.tensor.matmul(tile(KV, n), tile(k_tok, n), tile(v_toks[:, c.parity, :], n),
                                            start=True, stop=True)
                last.then_inc(kv_done, 1)
                if ln is not None:
                    pe.wait_ge(o_var_ready, rms + 1)
                    turn_xn(ln, late_banks)

            pe.wait_ge(xn_lo_done, KC * BLOCKS)
            for kk in range(PEELED):
                slot(0, kk)
            with pe.Fori(0, HEADS - LAST_HEADS) as i:
                for kk in range(PEELED, PEELED + BLOCKS):
                    slot(i, kk)
            for kk in range(PEELED, LAST_HEADS * BLOCKS):
                ln, rms = late_work(kk)
                slot(HEADS - LAST_HEADS, kk, ln, rms, before=KC * ln if ln else 0)

            def f_project(c, which, n, done):
                if c.tc == 0:
                    pe.wait_ge(w_ready[n], GROUPS + HEADS + c.head + 1)
                if c.later:
                    pe.wait_ge(f_mul, c.s - 1)
                project(f_banks(c)[which], n, c.tc).then_inc(done, 1)

            def f_down_product(p, turned=None):
                if p.tc == 0:
                    pe.wait_ge(w_ready["o"], GROUPS + HEADS + p.head + 1)
                pe.wait_ge(f_lo, p.done)
                if not p.first_ever:
                    pe.wait_ge(d_added, BT * p.s)
                for c in range(BT):
                    if turned is not None and c >= 2:
                        pe.wait_ge(xn_lo_done, KC * turned + c - 1)
                    product(y_bank[c][:, :], (o_hi, o_lo), (slice(None), slice(c * P, (c + 1) * P)),
                            (w_hi["o"], w_lo["o"]), (slice(None), slice(0, D)), True, True).then_inc(d_done, 1)

            def f_slot(i, kk, ln=None):
                c = Step(i, kk)
                pe.wait_ge(xn_lo_done, KC * (BLOCKS + c.tc + 1))
                f_project(c, 0, "k", fg_proj)
                if ln == BLOCKS + 2:
                    pe.wait_ge(o_var_ready, BLOCKS)
                f_project(c, 1, "g", fu_proj)
                if ln is not None:
                    pe.wait_ge(y_added, BT * STEPS)
                    pe.wait_ge(f_mul, c.s)
                    if c.later:
                        pe.wait_ge(d_added, BT * (c.s - 1))
                    turn_xn(ln, f_turn_banks(ln), by_tile=ln % BLOCKS == BLOCKS - 1)
                f_down_product(Step(i, kk - 1), ln)

            end, c = Step(HEADS - 1, BLOCKS - 1), Step(0, 0)
            f_project(c, 0, "k", fg_proj)
            output(end, before=KC * (BLOCKS + 2))
            pe.wait_ge(gate_done, STEPS)
            f_project(c, 1, "g", fu_proj)
            project_out(end)
            pe.wait_ge(k_tok_done, STEPS)
            pe.wait_ge(o_var_ready, BLOCKS - 1)
            sum_squares(BLOCKS - 1)
            f_slot(0, 1, ln=BLOCKS + 2)
            f_slot(0, 2, ln=BLOCKS + 3)
            with pe.Fori(0, CHUNKS - 1) as i:
                for kk in range(PEELED, PEELED + BLOCKS):
                    f_slot(i, kk)
            f_slot(CHUNKS - 1, BLOCKS - 1)
            f_down_product(Step(CHUNKS - 1, BLOCKS - 1))


def kernel(x, L0_tok_W, L0_tok_lora_A, L0_tok_lora_B, L0_attn_slope_rate, L0_attn_w_qkv, L0_attn_w_gate,
           L0_attn_w_out, L0_attn_norm_w, L0_ffn_w_gate, L0_ffn_w_up, L0_ffn_w_down):
    import concourse.bacc as bacc
    from concourse.bass_utils import run_bass_kernel_spmd

    def by_input(w):
        w = np.asarray(w)
        n = w.shape[0] // P
        return w.reshape(n, P, KC, P).transpose(0, 3, 2, 1).reshape(n, P, KC * P)

    qkv = np.asarray(L0_attn_w_qkv).reshape(HEADS, 3, P, D)
    v_w = qkv[:, 2].reshape(GROUPS, D, KC, P).transpose(0, 2, 3, 1)
    heads_w = np.stack([by_input(qkv[:, 1].reshape(INNER, D)), by_input(qkv[:, 0].reshape(INNER, D)),
                        by_input(L0_attn_w_gate), np.asarray(L0_attn_w_out).T.reshape(HEADS, P, D)], axis=1)
    arrays = {
        "ids": np.asarray(x).reshape(TILES, P).T,
        "table": np.asarray(L0_tok_W),
        "lora_a": np.asarray(L0_tok_lora_A).T,
        "lora_b": np.asarray(L0_tok_lora_B).T,
        "slopes": np.asarray(L0_attn_slope_rate).reshape(1, HEADS),
        "norm_w": np.asarray(L0_attn_norm_w).reshape(HEADS, P).T,
        "attn_w": np.concatenate([v_w, heads_w]),
        "ffn_w": np.stack([by_input(L0_ffn_w_gate), by_input(L0_ffn_w_up),
                           np.asarray(L0_ffn_w_down).T.reshape(CHUNKS, P, D)], axis=1),
    }
    arrays = {n: np.ascontiguousarray(a) for n, a in arrays.items()}
    nc = bacc.Bacc("TRN2", target_bir_lowering=False, num_devices=1)
    args = [nc.dram_tensor(n, a.shape, mybir.dt.from_np(a.dtype), kind="ExternalInput").ap()
            for n, a in arrays.items()]
    out = nc.dram_tensor("out", (T, D), F32, kind="ExternalOutput").ap()
    v_store = nc.dram_tensor("v_store", (HEADS, BLOCKS, P, BLOCK), F32, kind="Internal").ap()
    build(nc, *args, v_store, out)
    r = run_bass_kernel_spmd(nc, [arrays], core_ids=[0])
    return r.results[0]["out"].reshape(2, T // 2, D)
```
